# Optimizing a Trainium2 kernel written in Bass

```python
import numpy as np
import jax
import jax.numpy as jnp

def _softmax(x, axis=-1):
    return jax.nn.softmax(x, axis=axis)

def _gelu(x):
    return jax.nn.gelu(x, approximate=True)

def _silu(x):
    return jax.nn.silu(x)

def _sigmoid(x):
    return jax.nn.sigmoid(x)

def _layernorm(x, axis=-1, eps=1e-05):
    m = jnp.mean(x, axis=axis, keepdims=True)
    v = jnp.var(x, axis=axis, keepdims=True)
    return (x - m) / jnp.sqrt(v + eps)

def _scatter_add(tgt, idx, src, axis=0):
    return tgt.at[idx].add(src)

def _segment_sum(src, seg, n):
    return jax.ops.segment_sum(src, seg, n)
kernel_name = 'mk_gnn_resnorm_d2_gnn_r8_336cfc'

def setup_inputs(seed: int=0):
    np.random.seed(seed)
    _w = jnp.asarray

    def _rec_inputs():
        import jax
        import jax.numpy as jnp
        _gk = jax.random.key(seed)
        x = -0.000202 + 1 * jax.random.normal(jax.random.fold_in(_gk, 1), (12500, 64), jnp.float32)
        src = jax.random.randint(jax.random.fold_in(_gk, 2), (400000,), 0, 12500, jnp.int32)
        dst = jnp.minimum((12500 * jax.random.uniform(jax.random.fold_in(_gk, 3), (400000,)) ** 2.0).astype(jnp.int32), 99999)
        _o = jnp.argsort(dst, stable=True)
        src = src[_o]
        dst = dst[_o]
        edge_attr_64 = -2.25437e-05 + 0.999858 * jax.random.normal(jax.random.fold_in(_gk, 12), (400000, 64), jnp.float32)
        edge_type_32 = jax.random.randint(jax.random.fold_in(_gk, 13), (400000,), 0, 32, jnp.int32)
        return (x, src, dst, edge_attr_64, edge_type_32)
    x, src, dst, edge_attr_64, edge_type_32 = _rec_inputs()

    def _L0_gnn_setup():
        import jax, jax.numpy as jnp
        import numpy as np
        NEG_SLOPE = 0.01
        N, E, D, R = (12500, 125000, 64, 32)
        key = jax.random.key(seed)
        ks = jax.random.split(key, 8)
        return {'nfeat': jax.random.normal(ks[0], (N, D), dtype=jnp.float32), 'efeat': jax.random.normal(ks[1], (E, D), dtype=jnp.float32), 'src': jax.random.randint(ks[2], (E,), 0, N, dtype=jnp.int32), 'dst': jax.random.randint(ks[3], (E,), 0, N, dtype=jnp.int32), 'etype': jax.random.randint(ks[4], (E,), 0, R, dtype=jnp.int32), 'relation_weight': jax.random.normal(ks[5], (R, D, D), dtype=jnp.float32) * 0.05, 'res_w1': jax.random.normal(ks[6], (D, D), dtype=jnp.float32) * 0.05, 'res_w2': jax.random.normal(ks[7], (D, D), dtype=jnp.float32) * 0.05}
    _L0_gnn_all = _L0_gnn_setup()
    _L0_gnn_in = {k: v for k, v in _L0_gnn_all.items() if k in ('relation_weight', 'res_w1', 'res_w2')}
    del _L0_gnn_all

    def _L1_gnn_setup():
        import jax, jax.numpy as jnp
        import numpy as np
        key = jax.random.key(seed)
        k1, k2, k3 = jax.random.split(key, 3)
        N_SRC, N_DST, E, D = (12500, 12500, 200000, 64)
        h = jax.random.normal(k1, (N_SRC, D), dtype=jnp.float32)
        src_idx = jax.random.randint(k2, (E,), 0, N_SRC, dtype=jnp.int32)
        dst_idx = jax.random.randint(k3, (E,), 0, N_DST, dtype=jnp.int32)
        return {'h': h, 'src_idx': src_idx, 'dst_idx': dst_idx, 'num_src': N_SRC, 'num_dst': N_DST}
    _L1_gnn_all = _L1_gnn_setup()
    _L1_gnn_in = {k: v for k, v in _L1_gnn_all.items() if k in ()}
    del _L1_gnn_all
    return {'x': x, 'src': src, 'dst': dst, 'edge_attr_64': edge_attr_64, 'edge_type_32': edge_type_32, 'L0_gnn_relation_weight': _L0_gnn_in['relation_weight'], 'L0_gnn_res_w1': _L0_gnn_in['res_w1'], 'L0_gnn_res_w2': _L0_gnn_in['res_w2']}

def reference(x, src, dst, edge_attr_64, edge_type_32, L0_gnn_relation_weight, L0_gnn_res_w1, L0_gnn_res_w2):
    import jax
    import jax.numpy as jnp

    def _L0_gnn_ref(nfeat, efeat, src, dst, etype, relation_weight, res_w1, res_w2):
        import jax, jax.numpy as jnp
        import numpy as np
        NEG_SLOPE = 0.01
        N, D = nfeat.shape
        h = nfeat
        h_proj = jnp.einsum('nd,rde->rne', h, relation_weight)
        t_r = h_proj[etype, src]
        h_r = h_proj[etype, dst]
        att = jnp.sum(t_r * jnp.tanh(h_r + efeat), axis=-1)
        seg_max = jax.lax.stop_gradient(jax.ops.segment_max(att, dst, num_segments=N))
        att_exp = jnp.exp(att - seg_max[dst])
        denom = jax.ops.segment_sum(att_exp, dst, num_segments=N)
        a = att_exp / denom[dst]
        msg = h[src] * a[:, None]
        h_nb = jax.ops.segment_sum(msg, dst, num_segments=N)
        out = jax.nn.leaky_relu((h + h_nb) @ res_w1.T, NEG_SLOPE) + jax.nn.leaky_relu(h * h_nb @ res_w2.T, NEG_SLOPE)
        return out

    def _L1_gnn_ref(h, src_idx, dst_idx, num_src, num_dst):
        import jax, jax.numpy as jnp
        import numpy as np
        ones = jnp.ones(src_idx.shape[0], dtype=h.dtype)
        out_deg = jnp.clip(jax.ops.segment_sum(ones, src_idx, num_segments=num_src), 1.0)
        in_deg = jnp.clip(jax.ops.segment_sum(ones, dst_idx, num_segments=num_dst), 1.0)
        norm_src = out_deg ** (-1.0)
        norm_dst = in_deg ** (-1.0)
        feat_src = h * norm_src[:, None]
        msgs = feat_src[src_idx]
        rst = jax.ops.segment_sum(msgs, dst_idx, num_segments=num_dst)
        return rst * norm_dst[:, None]
    x = _layernorm(x + _L0_gnn_ref(x, edge_attr_64, src, dst, edge_type_32, L0_gnn_relation_weight, L0_gnn_res_w1, L0_gnn_res_w2), axis=-1)
    x = _layernorm(x + _L1_gnn_ref(x, src, dst, 12500, 12500), axis=-1)
    return x

_drawn_inputs = setup_inputs


def setup_inputs(seed=0):
    import zlib

    import numpy as np

    out = dict(_drawn_inputs(seed))
    spreads = {}
    factors = {}
    for name, (base, spread) in spreads.items():
        noise = np.random.default_rng([zlib.crc32(name.encode()), seed]).standard_normal(out[name].shape)
        drawn = base * np.exp(spread * noise) if base else spread * noise
        out[name] = jnp.asarray(drawn.astype(out[name].dtype))
    for name, factor in factors.items():
        out[name] = (out[name] * factor).astype(out[name].dtype)
    return out
```

```python
import concourse.bass as bass
from concourse import mybir
from contextlib import ExitStack

F32 = mybir.dt.float32
BF16 = mybir.dt.bfloat16
I32 = mybir.dt.int32
ALU = mybir.AluOpType
ACT = mybir.ActivationFunctionType
AX = mybir.AxisListType

P = 128
N, E, D, R = 12500, 400000, 64, 32
T = E // P
G = 25
CHUNKS = T // G
PAIRS = CHUNKS // 2
NB = -(-N // P)
NPAD = NB * P
TAILROWS = N - (NB - 1) * P
GB = 7
GROUPS = NB // GB
W = D + 1
RW = D + 2
BIG = 1.0e30
EPS = 1.0e-5
SLOPE = 0.01
assert T * P == E and G * CHUNKS == T and GB * GROUPS == NB and GROUPS % 2 == 0


def later(count):
    return not (isinstance(count, int) and count == 0)


class Steps:

    def __init__(self, engine, sem):
        self.engine, self.sem, self.base, self.n = engine, sem, 0, 0

    def at(self, base):
        self.base, self.n = base, 0

    def then(self, instruction):
        self.n += 1
        instruction.then_inc(self.sem, 1)
        self.engine.wait_ge(self.sem, self.base + self.n)


def tail_stage(nc, sb, ps, sem, dst_sb, head_next, iota_row, iota_col, ident, count_d, count_s,
               node_end, valid, key, tail):
    with ExitStack() as c:
        upto = sb(c, "upto", [P, P])
        after = sb(c, "after", [P, P])
        ones = sb(c, "ones", [P, P])
        wide = sb(c, "wide", [P, 2, P])
        group = sb(c, "group", [P, P])
        work = sb(c, "work", [P, P])
        total = sb(c, "total", [P, NB])
        before = sb(c, "before", [P, NB])
        goes_on = sb(c, "goes_on", [P, 1])
        small = sb(c, "small", [P, 4])
        ps_in = ps(c, "ps_in", [P, NB])
        ps_all = ps(c, "ps_all", [P, NB])
        ps_wide = ps(c, "ps_wide", [P, 2, P])
        vstep, ready, mm, ex_arg, ex_done = (sem(c, n) for n in ("vstep_t", "ready_t", "mm_t", "exarg_t", "exdone_t"))

        with nc.Block() as block:
            @block.vector
            def _(dve):
                link = Steps(dve, vstep)
                link.then(nc.vector.memset(ones[:, :], 1.0))
                link.then(nc.vector.tensor_scalar(upto[:, :], iota_row[:, 0:P], iota_col[:, 0:1], None, ALU.is_ge))
                link.then(nc.vector.tensor_scalar(after[:, :], iota_row[:, 0:P], iota_col[:, 0:1], None, ALU.is_gt))
                link.then(nc.vector.tensor_tensor(goes_on[:, :], dst_sb[:, T:T + 1], head_next[:, :], ALU.is_equal))
                link.then(nc.vector.tensor_scalar(small[:, 0:1], dst_sb[:, T:T + 1], 5.0, None, ALU.add))
                link.then(nc.vector.tensor_tensor(small[:, 1:2], small[:, 0:1], goes_on[:, :], ALU.mult))
                link.then(nc.vector.tensor_scalar(key[:, :], small[:, 1:2], -5.0, None, ALU.add))
                link.then(nc.vector.tensor_copy(wide[:, 0, :], key[:, 0:1].to_broadcast([P, P])))
                nc.vector.tensor_copy(wide[:, 1, :], tail[:, W:RW].to_broadcast([P, P])).then_inc(ready, 1)
                dve.wait_ge(mm, 1)
                link.then(nc.vector.tensor_copy(total[:, :], ps_all[:, :]))
                link.then(nc.vector.tensor_tensor_scan(before[:, :], ones[:, 0:NB], total[:, :], 0.0, ALU.mult, ALU.add))
                link.then(nc.vector.tensor_tensor(before[:, :], before[:, :], total[:, :], ALU.subtract))
                link.then(nc.vector.tensor_tensor(before[:, :], before[:, :], ps_in[:, :], ALU.add))
                link.then(nc.vector.tensor_scalar(node_end[:, :], before[:, :], -1.0, 0.0, ALU.add, ALU.max))
                link.then(nc.vector.tensor_scalar(valid[:, :], count_d[:, :], 1.0, None, ALU.min))
                link.then(nc.vector.tensor_scalar(count_d[:, :], count_d[:, :], 1.0, None, ALU.max))
                link.then(nc.vector.tensor_scalar(count_s[:, :], count_s[:, :], 1.0, None, ALU.max))
                link.then(nc.vector.reciprocal(count_d[:, :], count_d[:, :]))
                link.then(nc.vector.reciprocal(count_s[:, :], count_s[:, :]))
                link.then(nc.vector.tensor_scalar(group[:, :], ps_wide[:, 0, :], key[:, 0:1], None, ALU.is_equal))
                link.then(nc.vector.tensor_scalar(work[:, :], group[:, :], -1.0, BIG, ALU.add, ALU.mult))
                link.then(nc.vector.tensor_tensor(work[:, :], work[:, :], ps_wide[:, 1, :], ALU.add))
                link.then(nc.vector.tensor_reduce(small[:, 2:3], work[:, :], AX.X, ALU.max))
                nc.vector.tensor_tensor(small[:, 3:4], tail[:, W:RW], small[:, 2:3], ALU.subtract).then_inc(ex_arg, 1)
                link.then(nc.vector.tensor_tensor(work[:, :], group[:, :], after[:, :], ALU.mult))
                link.then(nc.vector.tensor_reduce(small[:, 0:1], work[:, :], AX.X, ALU.max))
                link.then(nc.vector.tensor_scalar(small[:, 0:1], small[:, 0:1], -1.0, 1.0, ALU.mult, ALU.add))
                link.then(nc.vector.tensor_tensor(tail[:, W:RW], small[:, 2:3], small[:, 0:1], ALU.mult))
                dve.wait_ge(ex_done, 1)
                link.then(nc.vector.tensor_scalar(tail[:, 0:W], tail[:, 0:W], small[:, 1:2], None, ALU.mult))

            @block.scalar
            def _(act):
                act.wait_ge(ex_arg, 1)
                nc.scalar.activation(small[:, 1:2], small[:, 3:4], ACT.Exp).then_inc(ex_done, 1)

            @block.tensor
            def _(pe):
                pe.wait_ge(ready, 1)
                nc.tensor.matmul(ps_in[:, :], upto[:, :], count_d[:, :], start=True, stop=True)
                nc.tensor.matmul(ps_all[:, :], ones[:, :], count_d[:, :], start=True, stop=True)
                nc.tensor.matmul(ps_wide[:, 0, :], wide[:, 0, :], ident[:, :], start=True, stop=True)
                nc.tensor.matmul(ps_wide[:, 1, :], wide[:, 1, :], ident[:, :], start=True, stop=True).then_inc(mm, 1)


def node_gathers(pool, pool_past, link_sem, idx, rows, rows_in, table):
    def gather(g, s):
        pool.wait_ge(link_sem, g + 1)
        pool.sem_inc(pool_past, 1)
        for b in range(GB):
            pool.indirect_dma_start(out=rows[:, s, b, :], out_offset=None, in_=table,
                                    in_offset=bass.IndirectOffsetOnAxis(ap=idx[:, s, b:b + 1], axis=0)).then_inc(rows_in[s], 16)

    with pool.Fori(0, GROUPS // 2) as i:
        gather(2 * i, 0)
        gather(2 * i + 1, 1)


def wide_of(v, n=D):
    return v.unsqueeze(2).to_broadcast([P, GB, n])


def attention_nodes(nc, sb, ps, sem, res_w1, res_w2, xs, ident, iota_row, pool_past, node_end, valid, key, tail,
                    count_s, sums0, ytab):
    with ExitStack() as c:
        idx = sb(c, "idx_n", [P, 2, GB], I32)
        rows = sb(c, "rows_n", [P, 2, GB, RW])
        mask = sb(c, "mask_n", [P, GB * P])
        shifted = sb(c, "shifted_n", [P, 1])
        carry = sb(c, "carry_n", [P, GB, RW])
        carry_max = sb(c, "carry_max", [P, GB])
        no_edge = sb(c, "no_edge", [P, NB])
        ex_in = sb(c, "ex_in_n", [P, 2, GB])
        ex = sb(c, "ex_n", [P, 2, GB])
        most = sb(c, "most", [P, GB])
        den = sb(c, "den", [P, GB])
        hnb = sb(c, "hnb", [P, GB, D])
        both = sb(c, "both", [P, GB, 2, D])
        bothT = sb(c, "bothT", [P, GB, P])
        part = sb(c, "part", [P, 2, GB, D])
        z = sb(c, "z", [P, GB, D])
        sq = sb(c, "sq", [P, GB, D])
        stat = sb(c, "stat", [P, 4, GB])
        y = sb(c, "y", [P, 2, GB, D])
        eps = sb(c, "eps", [P, 1])
        w_raw = sb(c, "w_raw", [D, 2, D])
        wT = sb(c, "wT", [P, D])
        ps_c = ps(c, "ps_c", [P, GB, RW])
        ps_t = [ps(c, f"ps_t{k}", [P, 4, P]) for k in range(2)]
        ps_o = [ps(c, f"ps_o{k}", [P, GB, D]) for k in range(2)]
        ps_w = ps(c, "ps_w", [P, D])
        rows_in = [sem(c, f"rows_in{s}") for s in range(2)]
        y_out = [sem(c, f"y_out{s}") for s in range(2)]
        staged, vstep, w_in = sem(c, "staged_n"), sem(c, "vstep_n"), sem(c, "w_in_n")
        mask_ready, carry_mm, carry_ready = sem(c, "mask_ready"), sem(c, "carry_mm"), sem(c, "carry_ready")
        ex_arg, ex_done = sem(c, "ex_arg_n"), sem(c, "ex_done_n")
        both_ready, both_t, bothT_ready = sem(c, "both_ready"), sem(c, "both_t"), sem(c, "bothT_ready")
        prod, part_ready = sem(c, "prod"), sem(c, "part_ready")
        var_ready, std_ready, y_ready = sem(c, "var_ready"), sem(c, "std_ready"), sem(c, "y_ready")
        w_mm, w_ready = sem(c, "w_mm"), sem(c, "w_ready")

        with nc.Block() as block:
            @block.sync
            def _(sp):
                sp.dma_start(w_raw[:, 0, :], res_w1).then_inc(w_in, 16)
                sp.dma_start(w_raw[:, 1, :], res_w2).then_inc(w_in, 16)

                def store(g, s):
                    sp.wait_ge(y_ready, g + 1)
                    sp.dma_start(ytab[bass.ds(g * GB * P, GB * P), :].rearrange("(b j) d -> j b d", j=P),
                                 y[:, s, :, :]).then_inc(y_out[s], 16)

                with sp.Fori(0, GROUPS // 2) as i:
                    store(2 * i, 0)
                    store(2 * i + 1, 1)
                for s in range(2):
                    sp.wait_ge(y_out[s], 16 * (GROUPS // 2))

            @block.gpsimd
            def _(pool):
                node_gathers(pool, pool_past, staged, idx, rows, rows_in, sums0)

            @block.vector
            def _(dve):
                link = Steps(dve, vstep)
                SETUP, PER_GROUP = 2, 23

                def stage(g, s):
                    at = bass.ds(g * GB, GB)
                    nc.vector.tensor_copy(idx[:, s, :], node_end[:, at]).then_inc(staged, 1)

                nc.vector.memset(eps[:, :], EPS)
                link.then(nc.vector.tensor_scalar(no_edge[:, :], valid[:, :], -1.0, 1.0, ALU.mult, ALU.add))
                link.then(nc.vector.tensor_copy(shifted[:, :], key[:, :]))
                stage(0, 0)
                stage(1, 1)

                def group(g, s, i, last):
                    link.at(SETUP + PER_GROUP * g)
                    at = bass.ds(g * GB, GB)
                    nc.vector.tensor_scalar(mask[:, :], iota_row[:, :], shifted[:, 0:1], None, ALU.is_equal).then_inc(mask_ready, 1)
                    dve.wait_ge(mask_ready, g + 1)
                    link.then(nc.vector.tensor_scalar(shifted[:, :], shifted[:, :], float(-GB * P), None, ALU.add))
                    dve.wait_ge(carry_ready, g + 1)
                    link.then(nc.vector.tensor_scalar(carry_max[:, :], carry[:, :, D], 0.0, None, ALU.is_gt))
                    link.then(nc.vector.tensor_scalar(carry_max[:, :], carry_max[:, :], -1.0, BIG, ALU.add, ALU.mult))
                    link.then(nc.vector.tensor_tensor(carry_max[:, :], carry_max[:, :], carry[:, :, W], ALU.add))
                    dve.wait_ge(rows_in[s], 16 * GB * (i + 1))
                    link.then(nc.vector.tensor_tensor(most[:, :], carry_max[:, :], rows[:, s, :, W], ALU.max))
                    link.then(nc.vector.tensor_tensor(ex_in[:, 0, :], rows[:, s, :, W], most[:, :], ALU.subtract))
                    nc.vector.tensor_tensor(ex_in[:, 1, :], carry_max[:, :], most[:, :], ALU.subtract).then_inc(ex_arg, 1)
                    dve.wait_ge(ex_done, g + 1)
                    link.then(nc.vector.tensor_tensor(ex[:, 0, :], ex[:, 0, :], valid[:, at], ALU.mult))
                    link.then(nc.vector.tensor_tensor(rows[:, s, :, 0:W], rows[:, s, :, 0:W], wide_of(ex[:, 0, :], W), ALU.mult))
                    link.then(nc.vector.tensor_tensor(carry[:, :, 0:W], carry[:, :, 0:W], wide_of(ex[:, 1, :], W), ALU.mult))
                    link.then(nc.vector.tensor_tensor(carry[:, :, 0:W], carry[:, :, 0:W], rows[:, s, :, 0:W], ALU.add))
                    if not last:
                        stage(g + 2, s)
                    link.then(nc.vector.tensor_tensor(den[:, :], carry[:, :, D], no_edge[:, at], ALU.add))
                    link.then(nc.vector.reciprocal(den[:, :], den[:, :]))
                    link.then(nc.vector.tensor_tensor(hnb[:, :, :], carry[:, :, 0:D], wide_of(den[:, :]), ALU.mult))
                    nc.vector.tensor_tensor(both[:, :, 0, :], xs[:, at, :], hnb[:, :, :], ALU.add)
                    nc.vector.tensor_tensor(both[:, :, 1, :], xs[:, at, :], hnb[:, :, :], ALU.mult).then_inc(both_ready, 1)
                    dve.wait_ge(part_ready, g + 1)
                    link.then(nc.vector.tensor_tensor(part[:, 0, :, :], part[:, 0, :, :], ps_o[0][:, :, :], ALU.max))
                    link.then(nc.vector.tensor_tensor(part[:, 1, :, :], part[:, 1, :, :], ps_o[1][:, :, :], ALU.max))
                    link.then(nc.vector.tensor_tensor(z[:, :, :], part[:, 0, :, :], part[:, 1, :, :], ALU.add))
                    link.then(nc.vector.tensor_tensor(z[:, :, :], z[:, :, :], xs[:, at, :], ALU.add))
                    layer_norm(g, at)
                    if later(i):
                        dve.wait_ge(y_out[s], 16 * i)
                    nc.vector.tensor_tensor(y[:, s, :, :], xs[:, at, :], wide_of(count_s[:, at]), ALU.mult).then_inc(y_ready, 1)
                    assert link.n == PER_GROUP, link.n

                def layer_norm(g, at):
                    link.then(nc.vector.tensor_reduce(stat[:, 0, :], z[:, :, :], AX.X, ALU.add))
                    link.then(nc.vector.tensor_scalar(stat[:, 0, :], stat[:, 0, :], 1.0 / D, None, ALU.mult))
                    link.then(nc.vector.tensor_tensor(z[:, :, :], z[:, :, :], wide_of(stat[:, 0, :]), ALU.subtract))
                    link.then(nc.vector.tensor_tensor(sq[:, :, :], z[:, :, :], z[:, :, :], ALU.mult))
                    nc.vector.tensor_reduce(stat[:, 1, :], sq[:, :, :], AX.X, ALU.add).then_inc(var_ready, 1)
                    dve.wait_ge(std_ready, g + 1)
                    link.then(nc.vector.reciprocal(stat[:, 3, :], stat[:, 2, :]))
                    link.then(nc.vector.tensor_tensor(xs[:, at, :], z[:, :, :], wide_of(stat[:, 3, :]), ALU.mult))

                group(0, 0, 0, False)
                group(1, 1, 0, False)
                with dve.Fori(1, GROUPS // 2 - 1) as i:
                    group(2 * i, 0, i, False)
                    group(2 * i + 1, 1, i, False)
                group(GROUPS - 2, 0, GROUPS // 2 - 1, True)
                group(GROUPS - 1, 1, GROUPS // 2 - 1, True)

            @block.scalar
            def _(act):
                for k in range(2):
                    act.wait_ge(w_mm, k + 1)
                    last = nc.scalar.copy(wT[64 * k:64 * k + D, :], ps_w[64 * k:64 * k + D, :])
                last.then_inc(w_ready, 1)
                def group(g):
                    act.wait_ge(carry_mm, g + 1)
                    if later(g):
                        act.wait_ge(both_ready, g)
                    nc.scalar.copy(carry[:, :, :], ps_c[:, :, :]).then_inc(carry_ready, 1)
                    act.wait_ge(ex_arg, g + 1)
                    nc.scalar.activation(ex[:, :, :], ex_in[:, :, :], ACT.Exp).then_inc(ex_done, 1)
                    act.wait_ge(both_t, g + 1)
                    nc.scalar.copy(bothT[:, 0:4, :], ps_t[0][:, :, :])
                    nc.scalar.copy(bothT[:, 4:GB, :], ps_t[1][:, 0:GB - 4, :]).then_inc(bothT_ready, 1)
                    act.wait_ge(prod, g + 1)
                    nc.scalar.mul(part[:, 0, :, :], ps_o[0][:, :, :], SLOPE)
                    nc.scalar.mul(part[:, 1, :, :], ps_o[1][:, :, :], SLOPE).then_inc(part_ready, 1)
                    act.wait_ge(var_ready, g + 1)
                    nc.scalar.activation(stat[:, 2, :], stat[:, 1, :], ACT.Sqrt, bias=eps[:, 0:1], scale=1.0 / D).then_inc(std_ready, 1)

                group(0)
                with act.Fori(1, GROUPS) as g:
                    group(g)

            @block.tensor
            def _(pe):
                pe.wait_ge(w_in, 32)
                nc.tensor.transpose(ps_w[0:D, :], w_raw[:, 0, :], ident[0:D, 0:D]).then_inc(w_mm, 1)
                pe.wait_ge(w_mm, 1)
                nc.tensor.matmul(ps_w[64:64 + D, :], w_raw[:, 1, :], ident[0:D, 0:D], start=True, stop=True).then_inc(w_mm, 1)
                pe.wait_ge(w_ready, 1)
                def group(g):
                    pe.wait_ge(mask_ready, g + 1)
                    if later(g):
                        pe.wait_ge(carry_ready, g)
                    for b in range(GB):
                        last = nc.tensor.matmul(ps_c[:, b, :], mask[:, b * P:(b + 1) * P], tail[:, :], start=True, stop=True)
                    last.then_inc(carry_mm, 1)
                    pe.wait_ge(both_ready, g + 1)
                    for b in range(GB):
                        last = nc.tensor.transpose(ps_t[b // 4][:, b % 4, :], both[:, b, :, :].rearrange("p a d -> p (a d)"), ident[:, :])
                    last.then_inc(both_t, 1)
                    pe.wait_ge(bothT_ready, g + 1)
                    for k in range(2):
                        for b in range(GB):
                            last = nc.tensor.matmul(ps_o[k][:, b, :], bothT[64 * k:64 * k + D, b, :], wT[64 * k:64 * k + D, :],
                                                    start=True, stop=True)
                    last.then_inc(prod, 1)

                group(0)
                with pe.Fori(1, GROUPS) as g:
                    group(g)


def mean_nodes(nc, sb, ps, sem, xs, iota_row, pool_past, node_end, valid, key, tail, count_d, sums1, out):
    with ExitStack() as c:
        idx = sb(c, "idx_m", [P, 2, GB], I32)
        rows = sb(c, "rows_m", [P, 2, GB, D])
        mask = sb(c, "mask_m", [P, GB * P])
        shifted = sb(c, "shifted_m", [P, 1])
        z = sb(c, "z_m", [P, GB, D])
        sq = sb(c, "sq_m", [P, GB, D])
        stat = sb(c, "stat_m", [P, 4, GB])
        y = sb(c, "y_m", [P, 2, GB, D])
        eps = sb(c, "eps_m", [P, 1])
        ps_c = ps(c, "ps_cm", [P, GB, D])
        rows_in = [sem(c, f"rows_inm{s}") for s in range(2)]
        y_out = [sem(c, f"y_outm{s}") for s in range(2)]
        staged, vstep = sem(c, "staged_m"), sem(c, "vstep_m")
        mask_ready, carry_mm, carry_used = sem(c, "mask_ready_m"), sem(c, "carry_mm_m"), sem(c, "carry_used_m")
        var_ready, std_ready, y_ready = sem(c, "var_ready_m"), sem(c, "std_ready_m"), sem(c, "y_ready_m")

        with nc.Block() as block:
            @block.sync
            def _(sp):
                def store(g, s):
                    sp.wait_ge(y_ready, g + 1)
                    sp.dma_start(out[bass.ds(g * GB * P, GB * P), :].rearrange("(b j) d -> j b d", j=P),
                                 y[:, s, :, :]).then_inc(y_out[s], 16)

                with sp.Fori(0, GROUPS // 2 - 1) as i:
                    store(2 * i, 0)
                    store(2 * i + 1, 1)
                store(GROUPS - 2, 0)
                sp.wait_ge(y_ready, GROUPS)
                n0 = (GROUPS - 1) * GB * P
                sp.dma_start(out[n0:n0 + (GB - 1) * P, :].rearrange("(b j) d -> j b d", j=P), y[:, 1, 0:GB - 1, :]).then_inc(y_out[1], 16)
                sp.dma_start(out[(NB - 1) * P:N, :], y[0:TAILROWS, 1, GB - 1, :]).then_inc(y_out[1], 16)
                sp.wait_ge(y_out[0], 16 * (GROUPS // 2))
                sp.wait_ge(y_out[1], 16 * (GROUPS // 2 + 1))

            @block.gpsimd
            def _(pool):
                node_gathers(pool, pool_past, staged, idx, rows, rows_in, sums1)

            @block.vector
            def _(dve):
                link = Steps(dve, vstep)
                SETUP, PER_GROUP = 1, 9

                def stage(g, s):
                    nc.vector.tensor_copy(idx[:, s, :], node_end[:, bass.ds(g * GB, GB)]).then_inc(staged, 1)

                nc.vector.memset(eps[:, :], EPS)
                link.then(nc.vector.tensor_copy(shifted[:, :], key[:, :]))
                stage(0, 0)
                stage(1, 1)

                def group(g, s, i, last):
                    link.at(SETUP + PER_GROUP * g)
                    at = bass.ds(g * GB, GB)
                    nc.vector.tensor_scalar(mask[:, :], iota_row[:, :], shifted[:, 0:1], None, ALU.is_equal).then_inc(mask_ready, 1)
                    dve.wait_ge(mask_ready, g + 1)
                    link.then(nc.vector.tensor_scalar(shifted[:, :], shifted[:, :], float(-GB * P), None, ALU.add))
                    dve.wait_ge(rows_in[s], 16 * GB * (i + 1))
                    link.then(nc.vector.tensor_tensor(z[:, :, :], rows[:, s, :, :], wide_of(valid[:, at]), ALU.mult))
                    if not last:
                        stage(g + 2, s)
                    dve.wait_ge(carry_mm, g + 1)
                    nc.vector.tensor_tensor(z[:, :, :], z[:, :, :], ps_c[:, :, :], ALU.add).then_inc(carry_used, 1)
                    dve.wait_ge(carry_used, g + 1)
                    link.then(nc.vector.tensor_tensor(z[:, :, :], z[:, :, :], wide_of(count_d[:, at]), ALU.mult))
                    link.then(nc.vector.tensor_tensor(z[:, :, :], z[:, :, :], xs[:, at, :], ALU.add))
                    link.then(nc.vector.tensor_reduce(stat[:, 0, :], z[:, :, :], AX.X, ALU.add))
                    link.then(nc.vector.tensor_scalar(stat[:, 0, :], stat[:, 0, :], 1.0 / D, None, ALU.mult))
                    link.then(nc.vector.tensor_tensor(z[:, :, :], z[:, :, :], wide_of(stat[:, 0, :]), ALU.subtract))
                    link.then(nc.vector.tensor_tensor(sq[:, :, :], z[:, :, :], z[:, :, :], ALU.mult))
                    nc.vector.tensor_reduce(stat[:, 1, :], sq[:, :, :], AX.X, ALU.add).then_inc(var_ready, 1)
                    dve.wait_ge(std_ready, g + 1)
                    link.then(nc.vector.reciprocal(stat[:, 3, :], stat[:, 2, :]))
                    if later(i):
                        dve.wait_ge(y_out[s], 16 * i)
                    nc.vector.tensor_tensor(y[:, s, :, :], z[:, :, :], wide_of(stat[:, 3, :]), ALU.mult).then_inc(y_ready, 1)
                    assert link.n == PER_GROUP, link.n

                group(0, 0, 0, False)
                group(1, 1, 0, False)
                with dve.Fori(1, GROUPS // 2 - 1) as i:
                    group(2 * i, 0, i, False)
                    group(2 * i + 1, 1, i, False)
                group(GROUPS - 2, 0, GROUPS // 2 - 1, True)
                group(GROUPS - 1, 1, GROUPS // 2 - 1, True)

            @block.scalar
            def _(act):
                def group(g):
                    act.wait_ge(var_ready, g + 1)
                    nc.scalar.activation(stat[:, 2, :], stat[:, 1, :], ACT.Sqrt, bias=eps[:, 0:1], scale=1.0 / D).then_inc(std_ready, 1)

                group(0)
                with act.Fori(1, GROUPS) as g:
                    group(g)

            @block.tensor
            def _(pe):
                def group(g):
                    pe.wait_ge(mask_ready, g + 1)
                    if later(g):
                        pe.wait_ge(carry_used, g)
                    for b in range(GB):
                        last = nc.tensor.matmul(ps_c[:, b, :], mask[:, b * P:(b + 1) * P], tail[:, 0:D], start=True, stop=True)
                    last.then_inc(carry_mm, 1)

                group(0)
                with pe.Fori(1, GROUPS) as g:
                    group(g)


def gnn_program(nc, x, src, dst, edge_attr, etype, rel_w, res_w1, res_w2, out):
    ctx = ExitStack()
    with ctx:
        def sb(c, name, shape, dt=F32):
            return c.enter_context(nc.sbuf_tensor(name, shape, dt))

        def ps(c, name, shape):
            return c.enter_context(nc.psum_tensor(name, shape, F32))

        def sem(c, name):
            return c.enter_context(nc.semaphore(name))

        table = nc.dram_tensor("table", (NPAD * R, 2 * D), F32).ap()
        sums0 = nc.dram_tensor("sums0", (E, RW), F32).ap()
        sums1 = nc.dram_tensor("sums1", (E, D), F32).ap()
        ytab = nc.dram_tensor("ytab", (NPAD, D), F32).ap()
        table_half = table.rearrange("a (b d) -> (a b) d", b=2)

        xs = sb(ctx, "xs", [P, NB, D])
        src_sb = sb(ctx, "src_sb", [P, T + 2 * G], I32)
        dst_sb = sb(ctx, "dst_sb", [P, 1 + T + 2 * G], I32)
        head_next = sb(ctx, "head_next", [P, 1], I32)
        iota_row = sb(ctx, "iota_row", [P, GB * P])
        iota_col = sb(ctx, "iota_col", [P, 1])
        ident = sb(ctx, "ident", [P, P])
        count_d = sb(ctx, "count_d", [P, NB])
        count_s = sb(ctx, "count_s", [P, NB])
        node_end = sb(ctx, "node_end", [P, NB], I32)
        valid = sb(ctx, "valid", [P, NB])
        key = sb(ctx, "key", [P, 1])
        tail = sb(ctx, "tail", [P, RW])

        with ExitStack() as c1:
            w_all = sb(c1, "w_all", [D, R, D])
            rows = sb(c1, "rows", [P, 2, R, 2 * D])
            xb = sb(c1, "xb", [P, D])
            xbT = sb(c1, "xbT", [D, 2, P])
            ps_x = ps(c1, "ps_x", [D, P])
            QUART = R * D // 4
            ps_p = [ps(c1, f"ps_p{k}", [P, QUART]) for k in range(4)]
            x_in, x_zero = sem(c1, "x_in"), sem(c1, "x_zero")
            w_in, idx_in, idx_pad = sem(c1, "w_in"), sem(c1, "idx_in"), sem(c1, "idx_pad")
            iota_done, const_done = sem(c1, "iota_done"), sem(c1, "const_done")
            xb_ready, xT_ready, xbT_ready = sem(c1, "xb_ready"), sem(c1, "xT_ready"), sem(c1, "xbT_ready")
            proj_ready = sem(c1, "proj_ready")
            taken = [sem(c1, f"taken{k}") for k in range(4)]
            dup_ready = sem(c1, "dup_ready")
            stored = [sem(c1, f"stored{s}") for s in range(2)]
            pool_past, pe_past = sem(ctx, "pool_past"), sem(c1, "pe_past")

            with nc.Block() as block:
                @block.sync
                def _(sp):
                    sp.wait_ge(x_zero, 1)
                    sp.dma_start(xs[:, 0:NB - 1, :], x[0:(NB - 1) * P, :].rearrange("(b j) d -> j b d", j=P)).then_inc(x_in, 16)
                    sp.dma_start(xs[0:TAILROWS, NB - 1, :], x[(NB - 1) * P:N, :]).then_inc(x_in, 16)
                    sp.dma_start(w_all[:, :, :], rel_w.rearrange("r d e -> d r e")).then_inc(w_in, 16)
                    sp.wait_ge(idx_pad, 4)
                    sp.dma_start(src_sb[:, 0:T], src.rearrange("(p t) -> p t", p=P)).then_inc(idx_in, 16)
                    sp.dma_start(dst_sb[:, 1:1 + T], dst.rearrange("(p t) -> p t", p=P)).then_inc(idx_in, 16)
                    with nc.allow_non_contiguous_dma(reason="one number of each partition"):
                        sp.dma_start(head_next[0:P - 1, :], dst[T:E].rearrange("(p t) -> p t", p=P - 1)[:, 0:1]).then_inc(idx_in, 16)

                    def store(b, s, i):
                        sp.wait_ge(dup_ready, b + 1)
                        for k in range(4):
                            sp.wait_ge(taken[k], b + 1)
                        sp.dma_start(table[bass.ds(b * P * R, P * R), :].rearrange("(j r) c -> j (r c)", r=R),
                                     rows[:, s, :, :].rearrange("p r c -> p (r c)")).then_inc(stored[s], 16)

                    with sp.Fori(0, NB // 2) as i:
                        store(2 * i, 0, i)
                        store(2 * i + 1, 1, i)
                    for s in range(2):
                        sp.wait_ge(stored[s], 16 * (NB // 2))
                    sp.wait_ge(idx_in, 48)

                @block.gpsimd
                def _(pool):
                    pool.iota(iota_row[:, :], [[1, GB * P]], base=0, channel_multiplier=0,
                              allow_small_or_imprecise_dtypes=True).then_inc(iota_done, 1)
                    pool.iota(iota_col[:, :], [[0, 1]], base=0, channel_multiplier=1,
                              allow_small_or_imprecise_dtypes=True).then_inc(iota_done, 1)
                    pool.wait_ge(x_in, 32)

                    def duplicate(b, s, i):
                        if later(b):
                            pool.wait_ge(xbT_ready, b)
                        pool.sem_inc(pool_past, 1)
                        pool.tensor_copy(xb[:, :], xs[:, bass.ds(b, 1), :].rearrange("p a d -> p (a d)")).then_inc(xb_ready, 1)
                        if later(i):
                            pool.wait_ge(stored[s], 16 * i)
                        pool.sem_inc(pool_past, 1)
                        pool.tensor_copy(rows[:, s, :, D:2 * D], xs[:, bass.ds(b, 1), :].to_broadcast([P, R, D])).then_inc(dup_ready, 1)

                    duplicate(0, 0, 0)
                    duplicate(1, 1, 0)
                    with pool.Fori(1, NB // 2) as i:
                        duplicate(2 * i, 0, i)
                        duplicate(2 * i + 1, 1, i)

                @block.tensor
                def _(pe):
                    pe.wait_ge(const_done, 1)
                    pe.wait_ge(w_in, 16)

                    def project(b, s, i):
                        pe.wait_ge(xb_ready, b + 1)
                        if later(b):
                            pe.wait_ge(xbT_ready, b)
                        pe.sem_inc(pe_past, 1)
                        nc.tensor.transpose(ps_x[:, :], xb[:, :], ident[:, :]).then_inc(xT_ready, 1)
                        pe.wait_ge(xbT_ready, b + 1)
                        for k in range(4):
                            if later(b):
                                pe.wait_ge(taken[k], b)
                            nc.tensor.matmul(ps_p[k][:, :], xbT[:, s, :],
                                             w_all[:, k * R // 4:(k + 1) * R // 4, :].rearrange("d r e -> d (r e)"),
                                             start=True, stop=True).then_inc(proj_ready, 1)

                    project(0, 0, 0)
                    project(1, 1, 0)
                    with pe.Fori(1, NB // 2) as i:
                        project(2 * i, 0, i)
                        project(2 * i + 1, 1, i)

                def take_out(engine, copy, k, b, s, i):
                    engine.wait_ge(proj_ready, 4 * b + k + 1)
                    if later(i):
                        engine.wait_ge(stored[s], 16 * i)
                    copy(rows[:, s, k * R // 4:(k + 1) * R // 4, 0:D],
                         ps_p[k][:, :].rearrange("p (r e) -> p r e", e=D)).then_inc(taken[k], 1)

                @block.vector
                def _(dve):
                    nc.vector.memset(xs[:, NB - 1, :], 0.0).then_inc(x_zero, 1)
                    nc.vector.memset(src_sb[:, T:], 0).then_inc(idx_pad, 1)
                    nc.vector.memset(dst_sb[:, 0:1], -1).then_inc(idx_pad, 1)
                    nc.vector.memset(dst_sb[:, 1 + T:], 0).then_inc(idx_pad, 1)
                    nc.vector.memset(head_next[:, :], -1).then_inc(idx_pad, 1)
                    dve.wait_ge(iota_done, 2)
                    nc.vector.tensor_scalar(ident[:, :], iota_row[:, 0:P], iota_col[:, 0:1], None, ALU.is_equal).then_inc(const_done, 1)

                    def quarters(b, s, i):
                        take_out(dve, nc.vector.tensor_copy, 0, b, s, i)
                        take_out(dve, nc.vector.tensor_copy, 2, b, s, i)

                    quarters(0, 0, 0)
                    quarters(1, 1, 0)
                    with dve.Fori(1, NB // 2) as i:
                        quarters(2 * i, 0, i)
                        quarters(2 * i + 1, 1, i)

                @block.scalar
                def _(act):
                    def quarters(b, s, i):
                        act.wait_ge(xT_ready, b + 1)
                        nc.scalar.copy(xbT[:, s, :], ps_x[:, :]).then_inc(xbT_ready, 1)
                        take_out(act, nc.scalar.copy, 1, b, s, i)
                        take_out(act, nc.scalar.copy, 3, b, s, i)

                    quarters(0, 0, 0)
                    quarters(1, 1, 0)
                    with act.Fori(1, NB // 2) as i:
                        quarters(2 * i, 0, i)
                        quarters(2 * i + 1, 1, i)

        with ExitStack() as c2:
            type_sb = sb(c2, "type_sb", [P, T + 2 * G], I32)
            idx_s = sb(c2, "idx_s", [P, 2, G], I32)
            idx_d = sb(c2, "idx_d", [P, 2, G], I32)
            gs = sb(c2, "gs", [P, 2, G, 2 * D])
            gd = sb(c2, "gd", [P, 2, G, D])
            ef = sb(c2, "ef", [P, 2, G, D])
            att = sb(c2, "att", [P, G])
            same = sb(c2, "same", [P, G])
            gap = sb(c2, "gap", [P, G])
            mx = sb(c2, "mx", [P, 1 + G])
            ex_in = sb(c2, "ex_in", [P, 2, G])
            ex = sb(c2, "ex", [P, 2, G])
            keep = sb(c2, "keep", [P, W, 1 + G])
            add = sb(c2, "add", [P, W, 1 + G])
            run = sb(c2, "run", [P, W, 1 + G])
            rowbuf = sb(c2, "rowbuf", [P, 2, G, RW])
            digit = sb(c2, "digit", [P, 4, G], I32)
            lo_s = sb(c2, "lo_s", [P, G, P], BF16)
            lo_d = sb(c2, "lo_d", [P, G, P], BF16)
            hi_s = sb(c2, "hi_s", [P, G, NB], BF16)
            hi_d = sb(c2, "hi_d", [P, G, NB], BF16)
            zero = sb(c2, "zero", [P, P], BF16)
            hist_s, hist_d = ps(c2, "hist_s", [P, NB]), ps(c2, "hist_d", [P, NB])
            type_in, type_pad = sem(c2, "type_in"), sem(c2, "type_pad")
            ef_in = [sem(c2, f"ef_in{s}") for s in range(2)]
            gs_in = [sem(c2, f"gs_in{s}") for s in range(2)]
            gd_in = [sem(c2, f"gd_in{s}") for s in range(2)]
            stored = [sem(c2, f"rows_stored{s}") for s in range(2)]
            vstep = sem(c2, "vstep")
            slot_ready = sem(c2, "slot_ready")
            tanh_arg, tanh_done = sem(c2, "tanh_arg"), sem(c2, "tanh_done")
            exp_arg, exp_done = sem(c2, "exp_arg"), sem(c2, "exp_done")
            keep_ready, run_ready, rows_ready = sem(c2, "keep_ready"), sem(c2, "run_ready"), sem(c2, "rows_ready")
            onehot_ready, onehot_used = sem(c2, "onehot_ready"), sem(c2, "onehot_used")
            hist_begun, hist_done, init_done = sem(c2, "hist_begun"), sem(c2, "hist_done"), sem(c2, "init_done")
            edges = edge_attr.rearrange("(p t) d -> p t d", p=P)
            sums0_v = sums0.rearrange("(p t) w -> p t w", p=P)

            with nc.Block() as block:
                @block.sync
                def _(sp):
                    sp.wait_ge(type_pad, 1)
                    sp.dma_start(type_sb[:, 0:T], etype.rearrange("(p t) -> p t", p=P)).then_inc(type_in, 16)

                    def load(c, s):
                        sp.dma_start(ef[:, s, :, :], edges[:, bass.ds(c * G, G), :]).then_inc(ef_in[s], 16)

                    load(0, 0)
                    load(1, 1)
                    with sp.Fori(0, PAIRS - 1) as i:
                        sp.wait_ge(tanh_arg, 2 * i + 1)
                        load(2 * i + 2, 0)
                        sp.wait_ge(tanh_arg, 2 * i + 2)
                        load(2 * i + 3, 1)
                    sp.wait_ge(tanh_arg, CHUNKS - 2)
                    load(CHUNKS - 1, 0)

                @block.gpsimd
                def _(pool):
                    def gather(c, s):
                        pool.wait_ge(slot_ready, c + 1)
                        pool.sem_inc(pool_past, 1)
                        for g in range(G):
                            pool.indirect_dma_start(
                                out=gs[:, s, g, :], out_offset=None, in_=table,
                                in_offset=bass.IndirectOffsetOnAxis(ap=idx_s[:, s, g:g + 1], axis=0)).then_inc(gs_in[s], 16)
                            pool.indirect_dma_start(
                                out=gd[:, s, g, :], out_offset=None, in_=table_half,
                                in_offset=bass.IndirectOffsetOnAxis(ap=idx_d[:, s, g:g + 1], axis=0)).then_inc(gd_in[s], 16)

                    with pool.Fori(0, PAIRS) as i:
                        gather(2 * i, 0)
                        gather(2 * i + 1, 1)
                    gather(CHUNKS - 1, 0)

                @block.vector
                def _(dve):
                    link = Steps(dve, vstep)
                    SETUP, PER_CHUNK = 6, 13

                    def stage(c, s):
                        at = bass.ds(c * G, G)
                        at_d = bass.ds(c * G + 1, G)
                        nc.vector.scalar_tensor_tensor(out=idx_s[:, s, :], in0=src_sb[:, at], scalar=float(R),
                                                       in1=type_sb[:, at], op0=ALU.mult, op1=ALU.add)
                        link.then(nc.vector.scalar_tensor_tensor(out=idx_d[:, s, :], in0=dst_sb[:, at_d], scalar=float(R),
                                                                 in1=type_sb[:, at], op0=ALU.mult, op1=ALU.add))
                        nc.vector.tensor_scalar(idx_d[:, s, :], idx_d[:, s, :], 2.0, None, ALU.mult).then_inc(slot_ready, 1)

                    nc.vector.memset(type_sb[:, T:], 0).then_inc(type_pad, 1)
                    nc.vector.memset(zero[:, :], 0.0).then_inc(init_done, 1)
                    link.then(nc.vector.memset(digit[:, :, :], 0))
                    link.then(nc.vector.memset(mx[:, :], -BIG))
                    link.then(nc.vector.memset(keep[:, :, :], 0.0))
                    link.then(nc.vector.memset(run[:, :, :], 0.0))
                    nc.vector.memset(add[:, :, :], 0.0).then_inc(init_done, 1)
                    dve.wait_ge(type_in, 16)
                    stage(0, 0)
                    stage(1, 1)
                    assert link.n == SETUP

                    def chunk(c, s, i):
                        link.at(SETUP + c * PER_CHUNK)
                        at = bass.ds(c * G, G)
                        at_d = bass.ds(c * G + 1, G)
                        dve.wait_ge(ef_in[s], 16 * (i + 1))
                        dve.wait_ge(gd_in[s], 16 * G * (i + 1))
                        nc.vector.tensor_tensor(gd[:, s, :, :], gd[:, s, :, :], ef[:, s, :, :], ALU.add).then_inc(tanh_arg, 1)
                        nc.vector.tensor_scalar(digit[:, 0, :], src_sb[:, at], 127, None, ALU.bitwise_and)
                        nc.vector.tensor_scalar(digit[:, 1, :], src_sb[:, at], 7, None, ALU.logical_shift_right)
                        nc.vector.tensor_scalar(digit[:, 2, :], dst_sb[:, at_d], 127, None, ALU.bitwise_and)
                        link.then(nc.vector.tensor_scalar(digit[:, 3, :], dst_sb[:, at_d], 7, None, ALU.logical_shift_right))
                        if later(c):
                            dve.wait_ge(onehot_used, c)
                        for k, (hot, width) in enumerate(((lo_s, P), (hi_s, NB), (lo_d, P), (hi_d, NB))):
                            last = nc.vector.tensor_tensor(
                                hot[:, :, :], iota_row[:, 0:width].unsqueeze(1).to_broadcast([P, G, width]),
                                digit[:, k, :].unsqueeze(2).to_broadcast([P, G, width]), ALU.is_equal)
                        last.then_inc(onehot_ready, 1)
                        link.then(nc.vector.tensor_tensor(same[:, :], dst_sb[:, at_d], dst_sb[:, at], ALU.is_equal))
                        link.then(nc.vector.tensor_scalar(gap[:, :], same[:, :], -1.0, BIG, ALU.add, ALU.mult))
                        dve.wait_ge(gs_in[s], 16 * G * (i + 1))
                        dve.wait_ge(tanh_done, c + 1)
                        link.then(nc.vector.tensor_tensor(gd[:, s, :, :], gd[:, s, :, :], gs[:, s, :, 0:D], ALU.mult))
                        link.then(nc.vector.tensor_reduce(att[:, :], gd[:, s, :, :], AX.X, ALU.add))
                        if later(c):
                            dve.wait_ge(rows_ready, c)
                        link.then(nc.vector.tensor_copy(mx[:, 0:1], mx[:, G:G + 1]))
                        link.then(nc.vector.tensor_tensor_scan(mx[:, 1:], gap[:, :], att[:, :], mx[:, 0:1], ALU.add, ALU.max))
                        link.then(nc.vector.tensor_tensor(ex_in[:, 0, :], att[:, :], mx[:, 1:], ALU.subtract))
                        link.then(nc.vector.tensor_tensor(ex_in[:, 1, :], mx[:, 0:G], gap[:, :], ALU.add))
                        nc.vector.tensor_tensor(ex_in[:, 1, :], ex_in[:, 1, :], mx[:, 1:], ALU.subtract).then_inc(exp_arg, 1)
                        link.then(nc.vector.tensor_copy(add[:, :, 0], run[:, :, G]))
                        dve.wait_ge(exp_done, c + 1)
                        link.then(nc.vector.tensor_copy(add[:, D, 1:], ex[:, 0, :]))
                        link.then(nc.vector.tensor_tensor(
                            add[:, 0:D, 1:].rearrange("p d t -> p t d"), gs[:, s, :, D:2 * D],
                            ex[:, 0, :].unsqueeze(2).to_broadcast([P, G, D]), ALU.mult))
                        dve.wait_ge(keep_ready, c + 1)
                        nc.vector.tensor_tensor_scan(run[:, :, :].rearrange("p w t -> p (w t)"),
                                                     keep[:, :, :].rearrange("p w t -> p (w t)"),
                                                     add[:, :, :].rearrange("p w t -> p (w t)"),
                                                     0.0, ALU.mult, ALU.add).then_inc(run_ready, 1)
                        stage(c + 2, s)
                        assert link.n == PER_CHUNK, link.n

                    chunk(0, 0, 0)
                    chunk(1, 1, 0)
                    with dve.Fori(1, PAIRS) as i:
                        chunk(2 * i, 0, i)
                        chunk(2 * i + 1, 1, i)
                    chunk(CHUNKS - 1, 0, PAIRS)
                    dve.wait_ge(hist_done, 1)
                    nc.vector.tensor_copy(count_s[:, :], hist_s[:, :])
                    nc.vector.tensor_copy(count_d[:, :], hist_d[:, :])
                    nc.vector.tensor_copy(tail[:, 0:W], run[:, :, G])
                    nc.vector.tensor_copy(tail[:, W:RW], mx[:, G:G + 1])

                @block.scalar
                def _(act):
                    act.wait_ge(init_done, 2)

                    def chunk(c, s, i):
                        act.wait_ge(tanh_arg, c + 1)
                        nc.scalar.activation(gd[:, s, :, :], gd[:, s, :, :], ACT.Tanh).then_inc(tanh_done, 1)
                        act.wait_ge(exp_arg, c + 1)
                        nc.scalar.activation(ex[:, :, :], ex_in[:, :, :], ACT.Exp).then_inc(exp_done, 1)
                        act.wait_ge(exp_done, c + 1)
                        nc.scalar.copy(keep[:, :, 1:], ex[:, 1, :].unsqueeze(1).to_broadcast([P, W, G])).then_inc(keep_ready, 1)
                        act.wait_ge(run_ready, c + 1)
                        if later(i):
                            act.wait_ge(stored[s], 16 * i)
                        nc.scalar.copy(rowbuf[:, s, :, 0:W], run[:, :, 1:].rearrange("p w t -> p t w"))
                        nc.scalar.copy(rowbuf[:, s, :, W], mx[:, 1:]).then_inc(rows_ready, 1)
                        act.wait_ge(rows_ready, c + 1)
                        act.dma_start(sums0_v[:, bass.ds(c * G, G), :], rowbuf[:, s, :, :]).then_inc(stored[s], 16)

                    chunk(0, 0, 0)
                    chunk(1, 1, 0)
                    with act.Fori(1, PAIRS) as i:
                        chunk(2 * i, 0, i)
                        chunk(2 * i + 1, 1, i)
                    chunk(CHUNKS - 1, 0, PAIRS)
                    act.wait_ge(stored[0], 16 * (PAIRS + 1))
                    act.wait_ge(stored[1], 16 * PAIRS)

                @block.tensor
                def _(pe):
                    pe.wait_ge(init_done, 1)
                    nc.tensor.matmul(hist_s[:, :], zero[:, :], zero[:, 0:NB], start=True, stop=False)
                    nc.tensor.matmul(hist_d[:, :], zero[:, :], zero[:, 0:NB], start=True, stop=False)
                    with pe.Fori(0, CHUNKS) as c:
                        pe.wait_ge(onehot_ready, c + 1)
                        for g in range(G):
                            nc.tensor.matmul(hist_s[:, :], lo_s[:, g, :], hi_s[:, g, :], start=False, stop=False)
                            last = nc.tensor.matmul(hist_d[:, :], lo_d[:, g, :], hi_d[:, g, :], start=False, stop=False)
                        last.then_inc(onehot_used, 1)
                    nc.tensor.matmul(hist_s[:, :], zero[:, :], zero[:, 0:NB], start=False, stop=True)
                    nc.tensor.matmul(hist_d[:, :], zero[:, :], zero[:, 0:NB], start=False, stop=True).then_inc(hist_done, 1)

        tail_stage(nc, sb, ps, sem, dst_sb, head_next, iota_row, iota_col, ident, count_d, count_s,
                   node_end, valid, key, tail)
        attention_nodes(nc, sb, ps, sem, res_w1, res_w2, xs, ident, iota_row, pool_past, node_end, valid, key, tail,
                        count_s, sums0, ytab)

        with ExitStack() as c4:
            idx = sb(c4, "idx", [P, 2, G], I32)
            gy = sb(c4, "gy", [P, 2, G, D])
            same = sb(c4, "same1", [P, G])
            keep = sb(c4, "keep1", [P, D, 1 + G])
            add = sb(c4, "add1", [P, D, 1 + G])
            run = sb(c4, "run1", [P, D, 1 + G])
            rowbuf = sb(c4, "rowbuf1", [P, 2, G, D])
            gy_in = [sem(c4, f"gy_in{s}") for s in range(2)]
            stored = [sem(c4, f"rows1_stored{s}") for s in range(2)]
            slot_ready, same_ready = sem(c4, "slot1_ready"), sem(c4, "same_ready")
            keep_ready, run_ready = sem(c4, "keep1_ready"), sem(c4, "run1_ready")
            rows_ready, init_done, vstep = sem(c4, "rows1_ready"), sem(c4, "init1_done"), sem(c4, "vstep1")
            sums1_v = sums1.rearrange("(p t) w -> p t w", p=P)

            with nc.Block() as block:
                @block.gpsimd
                def _(pool):
                    def gather(c, s):
                        pool.wait_ge(slot_ready, c + 1)
                        pool.sem_inc(pool_past, 1)
                        for g in range(G):
                            pool.indirect_dma_start(
                                out=gy[:, s, g, :], out_offset=None, in_=ytab,
                                in_offset=bass.IndirectOffsetOnAxis(ap=idx[:, s, g:g + 1], axis=0)).then_inc(gy_in[s], 16)

                    with pool.Fori(0, PAIRS) as i:
                        gather(2 * i, 0)
                        gather(2 * i + 1, 1)
                    gather(CHUNKS - 1, 0)

                @block.vector
                def _(dve):
                    link = Steps(dve, vstep)

                    def stage(c, s):
                        nc.vector.tensor_copy(idx[:, s, :], src_sb[:, bass.ds(c * G, G)]).then_inc(slot_ready, 1)

                    nc.vector.memset(keep[:, :, :], 0.0).then_inc(init_done, 1)
                    nc.vector.memset(add[:, :, :], 0.0).then_inc(init_done, 1)
                    link.then(nc.vector.memset(run[:, :, :], 0.0))
                    stage(0, 0)
                    stage(1, 1)

                    def chunk(c, s, i):
                        link.at(1 + c)
                        if later(c):
                            dve.wait_ge(keep_ready, c)
                        nc.vector.tensor_tensor(same[:, :], dst_sb[:, bass.ds(c * G + 1, G)], dst_sb[:, bass.ds(c * G, G)],
                                                ALU.is_equal).then_inc(same_ready, 1)
                        if later(c):
                            dve.wait_ge(rows_ready, c)
                        link.then(nc.vector.tensor_copy(add[:, :, 0], run[:, :, G]))
                        dve.wait_ge(gy_in[s], 16 * G * (i + 1))
                        dve.wait_ge(keep_ready, c + 1)
                        nc.vector.tensor_tensor_scan(run[:, :, :].rearrange("p w t -> p (w t)"),
                                                     keep[:, :, :].rearrange("p w t -> p (w t)"),
                                                     add[:, :, :].rearrange("p w t -> p (w t)"),
                                                     0.0, ALU.mult, ALU.add).then_inc(run_ready, 1)
                        stage(c + 2, s)

                    chunk(0, 0, 0)
                    chunk(1, 1, 0)
                    with dve.Fori(1, PAIRS) as i:
                        chunk(2 * i, 0, i)
                        chunk(2 * i + 1, 1, i)
                    chunk(CHUNKS - 1, 0, PAIRS)
                    dve.wait_ge(run_ready, CHUNKS)
                    nc.vector.tensor_copy(tail[:, 0:D], run[:, :, G])

                @block.scalar
                def _(act):
                    act.wait_ge(init_done, 2)

                    def chunk(c, s, i):
                        act.wait_ge(gy_in[s], 16 * G * (i + 1))
                        nc.scalar.copy(add[:, :, 1:].rearrange("p d t -> p t d"), gy[:, s, :, :])
                        act.wait_ge(same_ready, c + 1)
                        nc.scalar.copy(keep[:, :, 1:], same[:, :].unsqueeze(1).to_broadcast([P, D, G])).then_inc(keep_ready, 1)
                        act.wait_ge(run_ready, c + 1)
                        if later(i):
                            act.wait_ge(stored[s], 16 * i)
                        nc.scalar.copy(rowbuf[:, s, :, :], run[:, :, 1:].rearrange("p w t -> p t w")).then_inc(rows_ready, 1)
                        act.wait_ge(rows_ready, c + 1)
                        act.dma_start(sums1_v[:, bass.ds(c * G, G), :], rowbuf[:, s, :, :]).then_inc(stored[s], 16)

                    chunk(0, 0, 0)
                    chunk(1, 1, 0)
                    with act.Fori(1, PAIRS) as i:
                        chunk(2 * i, 0, i)
                        chunk(2 * i + 1, 1, i)
                    chunk(CHUNKS - 1, 0, PAIRS)
                    act.wait_ge(stored[0], 16 * (PAIRS + 1))
                    act.wait_ge(stored[1], 16 * PAIRS)

        mean_nodes(nc, sb, ps, sem, xs, iota_row, pool_past, node_end, valid, key, tail, count_d, sums1, out)


_INS = ['x', 'src', 'dst', 'edge_attr_64', 'edge_type_32', 'L0_gnn_relation_weight', 'L0_gnn_res_w1', 'L0_gnn_res_w2']
_OUTS = [((N, D), 'float32')]


def kernel(**inputs):
    import numpy as _np
    import concourse.bacc as _bacc
    from concourse import mybir as _mybir
    from concourse.bass_utils import run_bass_kernel_spmd as _run

    nc = _bacc.Bacc("TRN2", target_bir_lowering=False, num_devices=1)
    arrays, args = {}, []
    for name in _INS:
        a = _np.ascontiguousarray(inputs[name])
        arrays[f"in_{name}_dram"] = a
        args.append(nc.dram_tensor(f"in_{name}_dram", a.shape, _mybir.dt.from_np(a.dtype), kind="ExternalInput").ap())
    for i, (shape, dtype) in enumerate(_OUTS):
        dt = _mybir.dt.from_np(_np.dtype(dtype))
        args.append(nc.dram_tensor(f"out_{i}_dram", shape, dt, kind="ExternalOutput").ap())
    gnn_program(nc, *args)
    r = _run(nc, [arrays], core_ids=[0])
    return r.results[0]["out_0_dram"]
```

```python
import concourse.bass as bass
from concourse import mybir
from contextlib import ExitStack

F32 = mybir.dt.float32
BF16 = mybir.dt.bfloat16
I32 = mybir.dt.int32
ALU = mybir.AluOpType
ACT = mybir.ActivationFunctionType
AX = mybir.AxisListType

P = 128
N, E, D, R = 12500, 400000, 64, 32
T = E // P
G = 25
CHUNKS = T // G
PAIRS = CHUNKS // 2
NB = -(-N // P)
NPAD = NB * P
TAILROWS = N - (NB - 1) * P
GB = 7
GROUPS = NB // GB
W = D + 1
RW = D + 2
BIG = 1.0e30
EPS = 1.0e-5
SLOPE = 0.01
assert T * P == E and G * CHUNKS == T and GB * GROUPS == NB and GROUPS % 2 == 0


def later(count):
    return not (isinstance(count, int) and count == 0)


class Steps:

    def __init__(self, engine, sem):
        self.engine, self.sem, self.base, self.n = engine, sem, 0, 0

    def at(self, base):
        self.base, self.n = base, 0

    def then(self, instruction):
        self.n += 1
        instruction.then_inc(self.sem, 1)
        self.engine.wait_ge(self.sem, self.base + self.n)


def tail_stage(nc, sb, ps, sem, dst_sb, head_next, iota_row, iota_col, ident, count_d, count_s,
               node_end, valid, key, tail):
    with ExitStack() as c:
        upto = sb(c, "upto", [P, P])
        after = sb(c, "after", [P, P])
        ones = sb(c, "ones", [P, P])
        wide = sb(c, "wide", [P, 2, P])
        group = sb(c, "group", [P, P])
        work = sb(c, "work", [P, P])
        total = sb(c, "total", [P, NB])
        before = sb(c, "before", [P, NB])
        goes_on = sb(c, "goes_on", [P, 1])
        small = sb(c, "small", [P, 4])
        ps_in = ps(c, "ps_in", [P, NB])
        ps_all = ps(c, "ps_all", [P, NB])
        ps_wide = ps(c, "ps_wide", [P, 2, P])
        vstep, ready, mm, ex_arg, ex_done = (sem(c, n) for n in ("vstep_t", "ready_t", "mm_t", "exarg_t", "exdone_t"))

        with nc.Block() as block:
            @block.vector
            def _(dve):
                link = Steps(dve, vstep)
                link.then(nc.vector.memset(ones[:, :], 1.0))
                link.then(nc.vector.tensor_scalar(upto[:, :], iota_row[:, 0:P], iota_col[:, 0:1], None, ALU.is_ge))
                link.then(nc.vector.tensor_scalar(after[:, :], iota_row[:, 0:P], iota_col[:, 0:1], None, ALU.is_gt))
                link.then(nc.vector.tensor_tensor(goes_on[:, :], dst_sb[:, T:T + 1], head_next[:, :], ALU.is_equal))
                link.then(nc.vector.tensor_scalar(small[:, 0:1], dst_sb[:, T:T + 1], 5.0, None, ALU.add))
                link.then(nc.vector.tensor_tensor(small[:, 1:2], small[:, 0:1], goes_on[:, :], ALU.mult))
                link.then(nc.vector.tensor_scalar(key[:, :], small[:, 1:2], -5.0, None, ALU.add))
                link.then(nc.vector.tensor_copy(wide[:, 0, :], key[:, 0:1].to_broadcast([P, P])))
                nc.vector.tensor_copy(wide[:, 1, :], tail[:, W:RW].to_broadcast([P, P])).then_inc(ready, 1)
                dve.wait_ge(mm, 1)
                link.then(nc.vector.tensor_copy(total[:, :], ps_all[:, :]))
                link.then(nc.vector.tensor_tensor_scan(before[:, :], ones[:, 0:NB], total[:, :], 0.0, ALU.mult, ALU.add))
                link.then(nc.vector.tensor_tensor(before[:, :], before[:, :], total[:, :], ALU.subtract))
                link.then(nc.vector.tensor_tensor(before[:, :], before[:, :], ps_in[:, :], ALU.add))
                link.then(nc.vector.tensor_scalar(node_end[:, :], before[:, :], -1.0, 0.0, ALU.add, ALU.max))
                link.then(nc.vector.tensor_scalar(valid[:, :], count_d[:, :], 1.0, None, ALU.min))
                link.then(nc.vector.tensor_scalar(count_d[:, :], count_d[:, :], 1.0, None, ALU.max))
                link.then(nc.vector.tensor_scalar(count_s[:, :], count_s[:, :], 1.0, None, ALU.max))
                link.then(nc.vector.reciprocal(count_d[:, :], count_d[:, :]))
                link.then(nc.vector.reciprocal(count_s[:, :], count_s[:, :]))
                link.then(nc.vector.tensor_scalar(group[:, :], ps_wide[:, 0, :], key[:, 0:1], None, ALU.is_equal))
                link.then(nc.vector.tensor_scalar(work[:, :], group[:, :], -1.0, BIG, ALU.add, ALU.mult))
                link.then(nc.vector.tensor_tensor(work[:, :], work[:, :], ps_wide[:, 1, :], ALU.add))
                link.then(nc.vector.tensor_reduce(small[:, 2:3], work[:, :], AX.X, ALU.max))
                nc.vector.tensor_tensor(small[:, 3:4], tail[:, W:RW], small[:, 2:3], ALU.subtract).then_inc(ex_arg, 1)
                link.then(nc.vector.tensor_tensor(work[:, :], group[:, :], after[:, :], ALU.mult))
                link.then(nc.vector.tensor_reduce(small[:, 0:1], work[:, :], AX.X, ALU.max))
                link.then(nc.vector.tensor_scalar(small[:, 0:1], small[:, 0:1], -1.0, 1.0, ALU.mult, ALU.add))
                link.then(nc.vector.tensor_tensor(tail[:, W:RW], small[:, 2:3], small[:, 0:1], ALU.mult))
                dve.wait_ge(ex_done, 1)
                link.then(nc.vector.tensor_scalar(tail[:, 0:W], tail[:, 0:W], small[:, 1:2], None, ALU.mult))

            @block.scalar
            def _(act):
                act.wait_ge(ex_arg, 1)
                nc.scalar.activation(small[:, 1:2], small[:, 3:4], ACT.Exp).then_inc(ex_done, 1)

            @block.tensor
            def _(pe):
                pe.wait_ge(ready, 1)
                nc.tensor.matmul(ps_in[:, :], upto[:, :], count_d[:, :], start=True, stop=True)
                nc.tensor.matmul(ps_all[:, :], ones[:, :], count_d[:, :], start=True, stop=True)
                nc.tensor.matmul(ps_wide[:, 0, :], wide[:, 0, :], ident[:, :], start=True, stop=True)
                nc.tensor.matmul(ps_wide[:, 1, :], wide[:, 1, :], ident[:, :], start=True, stop=True).then_inc(mm, 1)


def node_gathers(pool, pool_past, link_sem, idx, rows, rows_in, table):
    def gather(g, s):
        pool.wait_ge(link_sem, g + 1)
        pool.sem_inc(pool_past, 1)
        for b in range(GB):
            pool.indirect_dma_start(out=rows[:, s, b, :], out_offset=None, in_=table,
                                    in_offset=bass.IndirectOffsetOnAxis(ap=idx[:, s, b:b + 1], axis=0)).then_inc(rows_in[s], 16)

    with pool.Fori(0, GROUPS // 2) as i:
        gather(2 * i, 0)
        gather(2 * i + 1, 1)


def wide_of(v, n=D):
    return v.unsqueeze(2).to_broadcast([P, GB, n])


def attention_nodes(nc, sb, ps, sem, res_w1, res_w2, xs, ident, iota_row, pool_past, node_end, valid, key, tail,
                    count_s, sums0, ytab):
    with ExitStack() as c:
        idx = sb(c, "idx_n", [P, 2, GB], I32)
        rows = sb(c, "rows_n", [P, 2, GB, RW])
        mask = sb(c, "mask_n", [P, 2, GB * P])
        shifted = sb(c, "shifted_n", [P, 1])
        carry = sb(c, "carry_n", [P, 2, GB, RW])
        carry_max = sb(c, "carry_max", [P, 2, GB])
        no_edge = sb(c, "no_edge", [P, NB])
        ex_in = sb(c, "ex_in_n", [P, 2, 2, GB])
        ex = sb(c, "ex_n", [P, 2, 2, GB])
        most = sb(c, "most", [P, 2, GB])
        den = sb(c, "den", [P, 2, GB])
        hnb = sb(c, "hnb", [P, 2, GB, D])
        both = sb(c, "both", [P, 2, GB, 2, D])
        bothT = sb(c, "bothT", [P, 2, GB, P])
        part = sb(c, "part", [P, 2, 2, GB, D])
        z = sb(c, "z", [P, 2, GB, D])
        sq = sb(c, "sq", [P, 2, GB, D])
        stat = sb(c, "stat", [P, 2, 4, GB])
        y = sb(c, "y", [P, 2, GB, D])
        eps = sb(c, "eps", [P, 1])
        w_raw = sb(c, "w_raw", [D, 2, D])
        wT = sb(c, "wT", [P, D])
        ps_c = [ps(c, f"ps_c{s}", [P, GB, RW]) for s in range(2)]
        ps_t = [ps(c, f"ps_t{k}", [P, 4, P]) for k in range(2)]
        ps_o = [[ps(c, f"ps_o{s}{k}", [P, GB, D]) for k in range(2)] for s in range(2)]
        ps_w = ps_c[0][:, 0, 0:D]
        rows_in = [sem(c, f"rows_in{s}") for s in range(2)]
        y_out = [sem(c, f"y_out{s}") for s in range(2)]
        staged, vstep, w_in = sem(c, "staged_n"), sem(c, "vstep_n"), sem(c, "w_in_n")
        mask_ready, carry_mm, carry_ready = sem(c, "mask_ready"), sem(c, "carry_mm"), sem(c, "carry_ready")
        ex_arg, ex_done, eps_ready = sem(c, "ex_arg_n"), sem(c, "ex_done_n"), sem(c, "eps_ready")
        both_ready, both_t, bothT_ready = sem(c, "both_ready"), sem(c, "both_t"), sem(c, "bothT_ready")
        prod, part_ready = sem(c, "prod"), sem(c, "part_ready")
        centred, sq_ready = sem(c, "centred"), sem(c, "sq_ready")
        var_ready, std_ready, y_ready = sem(c, "var_ready"), sem(c, "std_ready"), sem(c, "y_ready")
        w_mm, w_ready = sem(c, "w_mm"), sem(c, "w_ready")

        with nc.Block() as block:
            @block.sync
            def _(sp):
                sp.dma_start(w_raw[:, 0, :], res_w1).then_inc(w_in, 16)
                sp.dma_start(w_raw[:, 1, :], res_w2).then_inc(w_in, 16)

                def store(g, s):
                    sp.wait_ge(y_ready, g + 1)
                    sp.dma_start(ytab[bass.ds(g * GB * P, GB * P), :].rearrange("(b j) d -> j b d", j=P),
                                 y[:, s, :, :]).then_inc(y_out[s], 16)

                with sp.Fori(0, GROUPS // 2) as i:
                    store(2 * i, 0)
                    store(2 * i + 1, 1)
                for s in range(2):
                    sp.wait_ge(y_out[s], 16 * (GROUPS // 2))

            @block.gpsimd
            def _(pool):
                node_gathers(pool, pool_past, staged, idx, rows, rows_in, sums0)

            @block.vector
            def _(dve):
                link = Steps(dve, vstep)
                SETUP, FRONT, BACK = 2, 2 * 11, 2 * 7

                def stage(g, s):
                    nc.vector.tensor_copy(idx[:, s, :], node_end[:, bass.ds(g * GB, GB)]).then_inc(staged, 1)

                nc.vector.memset(eps[:, :], EPS).then_inc(eps_ready, 1)
                link.then(nc.vector.tensor_scalar(no_edge[:, :], valid[:, :], -1.0, 1.0, ALU.mult, ALU.add))
                link.then(nc.vector.tensor_copy(shifted[:, :], key[:, :]))
                stage(0, 0)
                stage(1, 1)

                def masks(g, s, i, last):
                    nc.vector.tensor_scalar(mask[:, s, :], iota_row[:, :], shifted[:, 0:1], None, ALU.is_equal).then_inc(mask_ready, 1)
                    dve.wait_ge(mask_ready, g + 1)
                    link.then(nc.vector.tensor_scalar(shifted[:, :], shifted[:, :], float(-GB * P), None, ALU.add))

                def maxima(g, s, i, last):
                    dve.wait_ge(carry_ready, g + 1)
                    link.then(nc.vector.tensor_scalar(carry_max[:, s, :], carry[:, s, :, D], 0.0, None, ALU.is_gt))
                    link.then(nc.vector.tensor_scalar(carry_max[:, s, :], carry_max[:, s, :], -1.0, BIG, ALU.add, ALU.mult))
                    link.then(nc.vector.tensor_tensor(carry_max[:, s, :], carry_max[:, s, :], carry[:, s, :, W], ALU.add))
                    dve.wait_ge(rows_in[s], 16 * GB * (i + 1))
                    link.then(nc.vector.tensor_tensor(most[:, s, :], carry_max[:, s, :], rows[:, s, :, W], ALU.max))
                    nc.vector.tensor_tensor(ex_in[:, s, 0, :], rows[:, s, :, W], most[:, s, :], ALU.subtract)
                    nc.vector.tensor_tensor(ex_in[:, s, 1, :], carry_max[:, s, :], most[:, s, :], ALU.subtract).then_inc(ex_arg, 1)

                def neighbours(g, s, i, last):
                    at = bass.ds(g * GB, GB)
                    dve.wait_ge(ex_done, g + 1)
                    link.then(nc.vector.tensor_tensor(ex[:, s, 0, :], ex[:, s, 0, :], valid[:, at], ALU.mult))
                    nc.vector.tensor_tensor(rows[:, s, :, 0:W], rows[:, s, :, 0:W], wide_of(ex[:, s, 0, :], W), ALU.mult)
                    link.then(nc.vector.tensor_tensor(carry[:, s, :, 0:W], carry[:, s, :, 0:W], wide_of(ex[:, s, 1, :], W), ALU.mult))
                    link.then(nc.vector.tensor_tensor(carry[:, s, :, 0:W], carry[:, s, :, 0:W], rows[:, s, :, 0:W], ALU.add))
                    if not last:
                        stage(g + 2, s)
                    link.then(nc.vector.tensor_tensor(den[:, s, :], carry[:, s, :, D], no_edge[:, at], ALU.add))
                    link.then(nc.vector.reciprocal(den[:, s, :], den[:, s, :]))
                    link.then(nc.vector.tensor_tensor(hnb[:, s, :, :], carry[:, s, :, 0:D], wide_of(den[:, s, :]), ALU.mult))
                    nc.vector.tensor_tensor(both[:, s, :, 0, :], xs[:, at, :], hnb[:, s, :, :], ALU.add)
                    nc.vector.tensor_tensor(both[:, s, :, 1, :], xs[:, at, :], hnb[:, s, :, :], ALU.mult).then_inc(both_ready, 1)

                def residual(g, s, i, last):
                    at = bass.ds(g * GB, GB)
                    dve.wait_ge(part_ready, g + 1)
                    for k in range(2):
                        last_max = nc.vector.tensor_tensor(part[:, s, k, :, :], part[:, s, k, :, :], ps_o[s][k][:, :, :], ALU.max)
                    link.then(last_max)
                    link.then(nc.vector.tensor_tensor(z[:, s, :, :], part[:, s, 0, :, :], part[:, s, 1, :, :], ALU.add))
                    link.then(nc.vector.tensor_tensor(z[:, s, :, :], z[:, s, :, :], xs[:, at, :], ALU.add))
                    link.then(nc.vector.tensor_reduce(stat[:, s, 0, :], z[:, s, :, :], AX.X, ALU.add))
                    link.then(nc.vector.tensor_scalar(stat[:, s, 0, :], stat[:, s, 0, :], 1.0 / D, None, ALU.mult))
                    nc.vector.tensor_tensor(z[:, s, :, :], z[:, s, :, :], wide_of(stat[:, s, 0, :]), ALU.subtract).then_inc(centred, 1)

                def variance(g, s, i, last):
                    dve.wait_ge(sq_ready, g + 1)
                    nc.vector.tensor_reduce(stat[:, s, 1, :], sq[:, s, :, :], AX.X, ALU.add).then_inc(var_ready, 1)

                def normed(g, s, i, last):
                    at = bass.ds(g * GB, GB)
                    dve.wait_ge(std_ready, g + 1)
                    link.then(nc.vector.reciprocal(stat[:, s, 3, :], stat[:, s, 2, :]))
                    link.then(nc.vector.tensor_tensor(xs[:, at, :], z[:, s, :, :], wide_of(stat[:, s, 3, :]), ALU.mult))
                    if later(i):
                        dve.wait_ge(y_out[s], 16 * i)
                    nc.vector.tensor_tensor(y[:, s, :, :], xs[:, at, :], wide_of(count_s[:, at]), ALU.mult).then_inc(y_ready, 1)

                def turn(i, front, back, last=False):
                    link.at(SETUP if not back else SETUP + FRONT + (FRONT + BACK) * (i - 1))
                    for first, second in ((masks, residual), (maxima, variance), (neighbours, normed)):
                        if front:
                            first(2 * i, 0, i, last)
                            first(2 * i + 1, 1, i, last)
                        if back:
                            second(2 * i - 2, 0, i - 1, last)
                            second(2 * i - 1, 1, i - 1, last)
                    assert link.n == FRONT * front + BACK * back, link.n

                pairs = GROUPS // 2
                turn(0, True, False)
                turn(1, True, True)
                with dve.Fori(2, pairs - 1) as i:
                    turn(i, True, True)
                turn(pairs - 1, True, True, last=True)
                turn(pairs, False, True)

            @block.scalar
            def _(act):
                for k in range(2):
                    act.wait_ge(w_mm, k + 1)
                    last = nc.scalar.copy(wT[64 * k:64 * k + D, :], ps_w[64 * k:64 * k + D, :])
                last.then_inc(w_ready, 1)
                act.wait_ge(eps_ready, 1)

                def carries(g, s):
                    act.wait_ge(carry_mm, g + 1)
                    nc.scalar.copy(carry[:, s, :, :], ps_c[s][:, :, :]).then_inc(carry_ready, 1)

                def exps(g, s):
                    act.wait_ge(ex_arg, g + 1)
                    nc.scalar.activation(ex[:, s, :, :], ex_in[:, s, :, :], ACT.Exp).then_inc(ex_done, 1)

                def transposed(g, s):
                    act.wait_ge(both_t, g + 1)
                    nc.scalar.copy(bothT[:, s, 0:4, :], ps_t[0][:, :, :])
                    nc.scalar.copy(bothT[:, s, 4:GB, :], ps_t[1][:, 0:GB - 4, :]).then_inc(bothT_ready, 1)

                def leaky(g, s):
                    act.wait_ge(prod, g + 1)
                    nc.scalar.mul(part[:, s, 0, :, :], ps_o[s][0][:, :, :], SLOPE)
                    nc.scalar.mul(part[:, s, 1, :, :], ps_o[s][1][:, :, :], SLOPE).then_inc(part_ready, 1)

                def squares(g, s):
                    act.wait_ge(centred, g + 1)
                    nc.scalar.activation(sq[:, s, :, :], z[:, s, :, :], ACT.Square).then_inc(sq_ready, 1)

                def deviations(g, s):
                    act.wait_ge(var_ready, g + 1)
                    nc.scalar.activation(stat[:, s, 2, :], stat[:, s, 1, :], ACT.Sqrt, bias=eps[:, 0:1], scale=1.0 / D).then_inc(std_ready, 1)

                def turn(i, front, back):
                    for first, second in ((carries, squares), (exps, deviations), (transposed, None), (leaky, None)):
                        if front:
                            first(2 * i, 0)
                            first(2 * i + 1, 1)
                        if back and second:
                            second(2 * i - 2, 0)
                            second(2 * i - 1, 1)

                pairs = GROUPS // 2
                turn(0, True, False)
                with act.Fori(1, pairs) as i:
                    turn(i, True, True)
                turn(pairs, False, True)

            @block.tensor
            def _(pe):
                pe.wait_ge(w_in, 32)
                nc.tensor.transpose(ps_w[0:D, :], w_raw[:, 0, :], ident[0:D, 0:D]).then_inc(w_mm, 1)
                pe.wait_ge(w_mm, 1)
                nc.tensor.matmul(ps_w[64:64 + D, :], w_raw[:, 1, :], ident[0:D, 0:D], start=True, stop=True).then_inc(w_mm, 1)
                pe.wait_ge(w_ready, 1)

                def carries(g, s):
                    pe.wait_ge(mask_ready, g + 1)
                    for b in range(GB):
                        last = nc.tensor.matmul(ps_c[s][:, b, :], mask[:, s, b * P:(b + 1) * P], tail[:, :], start=True, stop=True)
                    last.then_inc(carry_mm, 1)

                def transposes(g, s):
                    pe.wait_ge(both_ready, g + 1)
                    if later(g):
                        pe.wait_ge(bothT_ready, g)
                    for b in range(GB):
                        last = nc.tensor.transpose(ps_t[b // 4][:, b % 4, :], both[:, s, b, :, :].rearrange("p a d -> p (a d)"), ident[:, :])
                    last.then_inc(both_t, 1)

                def products(g, s):
                    pe.wait_ge(bothT_ready, g + 1)
                    for k in range(2):
                        for b in range(GB):
                            last = nc.tensor.matmul(ps_o[s][k][:, b, :], bothT[64 * k:64 * k + D, s, b, :], wT[64 * k:64 * k + D, :],
                                                    start=True, stop=True)
                    last.then_inc(prod, 1)

                def pair(i):
                    for step in (carries, transposes, products):
                        step(2 * i, 0)
                        step(2 * i + 1, 1)

                pair(0)
                with pe.Fori(1, GROUPS // 2) as i:
                    pair(i)


def mean_nodes(nc, sb, ps, sem, xs, iota_row, pool_past, node_end, valid, key, tail, count_d, sums1, out):
    with ExitStack() as c:
        idx = sb(c, "idx_m", [P, 2, GB], I32)
        rows = sb(c, "rows_m", [P, 2, GB, D])
        mask = sb(c, "mask_m", [P, 2, GB * P])
        shifted = sb(c, "shifted_m", [P, 1])
        z = sb(c, "z_m", [P, 2, GB, D])
        sq = sb(c, "sq_m", [P, 2, GB, D])
        stat = sb(c, "stat_m", [P, 2, 4, GB])
        y = sb(c, "y_m", [P, 2, GB, D])
        eps = sb(c, "eps_m", [P, 1])
        ps_c = [ps(c, f"ps_cm{s}", [P, GB, D]) for s in range(2)]
        rows_in = [sem(c, f"rows_inm{s}") for s in range(2)]
        y_out = [sem(c, f"y_outm{s}") for s in range(2)]
        staged, vstep, eps_ready = sem(c, "staged_m"), sem(c, "vstep_m"), sem(c, "eps_ready_m")
        mask_ready, carry_mm = sem(c, "mask_ready_m"), sem(c, "carry_mm_m")
        centred, sq_ready = sem(c, "centred_m"), sem(c, "sq_ready_m")
        var_ready, std_ready, y_ready = sem(c, "var_ready_m"), sem(c, "std_ready_m"), sem(c, "y_ready_m")

        with nc.Block() as block:
            @block.sync
            def _(sp):
                def store(g, s):
                    sp.wait_ge(y_ready, g + 1)
                    sp.dma_start(out[bass.ds(g * GB * P, GB * P), :].rearrange("(b j) d -> j b d", j=P),
                                 y[:, s, :, :]).then_inc(y_out[s], 16)

                with sp.Fori(0, GROUPS // 2 - 1) as i:
                    store(2 * i, 0)
                    store(2 * i + 1, 1)
                store(GROUPS - 2, 0)
                sp.wait_ge(y_ready, GROUPS)
                n0 = (GROUPS - 1) * GB * P
                sp.dma_start(out[n0:n0 + (GB - 1) * P, :].rearrange("(b j) d -> j b d", j=P), y[:, 1, 0:GB - 1, :]).then_inc(y_out[1], 16)
                sp.dma_start(out[(NB - 1) * P:N, :], y[0:TAILROWS, 1, GB - 1, :]).then_inc(y_out[1], 16)
                sp.wait_ge(y_out[0], 16 * (GROUPS // 2))
                sp.wait_ge(y_out[1], 16 * (GROUPS // 2 + 1))

            @block.gpsimd
            def _(pool):
                node_gathers(pool, pool_past, staged, idx, rows, rows_in, sums1)

            @block.vector
            def _(dve):
                link = Steps(dve, vstep)
                SETUP, PER_PAIR = 1, 2 * 8

                def stage(g, s):
                    nc.vector.tensor_copy(idx[:, s, :], node_end[:, bass.ds(g * GB, GB)]).then_inc(staged, 1)

                nc.vector.memset(eps[:, :], EPS).then_inc(eps_ready, 1)
                link.then(nc.vector.tensor_copy(shifted[:, :], key[:, :]))
                stage(0, 0)
                stage(1, 1)

                def masks(g, s, i, last):
                    nc.vector.tensor_scalar(mask[:, s, :], iota_row[:, :], shifted[:, 0:1], None, ALU.is_equal).then_inc(mask_ready, 1)
                    dve.wait_ge(mask_ready, g + 1)
                    link.then(nc.vector.tensor_scalar(shifted[:, :], shifted[:, :], float(-GB * P), None, ALU.add))

                def residual(g, s, i, last):
                    at = bass.ds(g * GB, GB)
                    dve.wait_ge(rows_in[s], 16 * GB * (i + 1))
                    link.then(nc.vector.tensor_tensor(z[:, s, :, :], rows[:, s, :, :], wide_of(valid[:, at]), ALU.mult))
                    if not last:
                        stage(g + 2, s)
                    dve.wait_ge(carry_mm, g + 1)
                    link.then(nc.vector.tensor_tensor(z[:, s, :, :], z[:, s, :, :], ps_c[s][:, :, :], ALU.add))
                    link.then(nc.vector.tensor_tensor(z[:, s, :, :], z[:, s, :, :], wide_of(count_d[:, at]), ALU.mult))
                    link.then(nc.vector.tensor_tensor(z[:, s, :, :], z[:, s, :, :], xs[:, at, :], ALU.add))
                    link.then(nc.vector.tensor_reduce(stat[:, s, 0, :], z[:, s, :, :], AX.X, ALU.add))
                    link.then(nc.vector.tensor_scalar(stat[:, s, 0, :], stat[:, s, 0, :], 1.0 / D, None, ALU.mult))
                    nc.vector.tensor_tensor(z[:, s, :, :], z[:, s, :, :], wide_of(stat[:, s, 0, :]), ALU.subtract).then_inc(centred, 1)

                def variance(g, s, i, last):
                    dve.wait_ge(sq_ready, g + 1)
                    nc.vector.tensor_reduce(stat[:, s, 1, :], sq[:, s, :, :], AX.X, ALU.add).then_inc(var_ready, 1)

                def normed(g, s, i, last):
                    dve.wait_ge(std_ready, g + 1)
                    link.then(nc.vector.reciprocal(stat[:, s, 3, :], stat[:, s, 2, :]))
                    if later(i):
                        dve.wait_ge(y_out[s], 16 * i)
                    nc.vector.tensor_tensor(y[:, s, :, :], z[:, s, :, :], wide_of(stat[:, s, 3, :]), ALU.mult).then_inc(y_ready, 1)

                def pair(i, last):
                    link.at(SETUP + PER_PAIR * i)
                    for step in (masks, residual, variance, normed):
                        step(2 * i, 0, i, last)
                        step(2 * i + 1, 1, i, last)
                    assert link.n == PER_PAIR, link.n

                pair(0, False)
                with dve.Fori(1, GROUPS // 2 - 1) as i:
                    pair(i, False)
                pair(GROUPS // 2 - 1, True)

            @block.scalar
            def _(act):
                act.wait_ge(eps_ready, 1)

                def squares(g, s):
                    act.wait_ge(centred, g + 1)
                    nc.scalar.activation(sq[:, s, :, :], z[:, s, :, :], ACT.Square).then_inc(sq_ready, 1)

                def deviations(g, s):
                    act.wait_ge(var_ready, g + 1)
                    nc.scalar.activation(stat[:, s, 2, :], stat[:, s, 1, :], ACT.Sqrt, bias=eps[:, 0:1], scale=1.0 / D).then_inc(std_ready, 1)

                with act.Fori(0, GROUPS // 2) as i:
                    for step in (squares, deviations):
                        step(2 * i, 0)
                        step(2 * i + 1, 1)

            @block.tensor
            def _(pe):
                def carries(g, s):
                    pe.wait_ge(mask_ready, g + 1)
                    for b in range(GB):
                        last = nc.tensor.matmul(ps_c[s][:, b, :], mask[:, s, b * P:(b + 1) * P], tail[:, 0:D], start=True, stop=True)
                    last.then_inc(carry_mm, 1)

                with pe.Fori(0, GROUPS // 2) as i:
                    carries(2 * i, 0)
                    carries(2 * i + 1, 1)


def gnn_program(nc, x, src, dst, edge_attr, etype, rel_w, res_w1, res_w2, out):
    ctx = ExitStack()
    with ctx:
        def sb(c, name, shape, dt=F32):
            return c.enter_context(nc.sbuf_tensor(name, shape, dt))

        def ps(c, name, shape):
            return c.enter_context(nc.psum_tensor(name, shape, F32))

        def sem(c, name):
            return c.enter_context(nc.semaphore(name))

        table = nc.dram_tensor("table", (NPAD * R, 2 * D), F32).ap()
        sums0 = nc.dram_tensor("sums0", (E, RW), F32).ap()
        sums1 = nc.dram_tensor("sums1", (E, D), F32).ap()
        ytab = nc.dram_tensor("ytab", (NPAD, D), F32).ap()
        table_half = table.rearrange("a (b d) -> (a b) d", b=2)

        xs = sb(ctx, "xs", [P, NB, D])
        src_sb = sb(ctx, "src_sb", [P, T + 2 * G], I32)
        dst_sb = sb(ctx, "dst_sb", [P, 1 + T + 2 * G], I32)
        head_next = sb(ctx, "head_next", [P, 1], I32)
        iota_row = sb(ctx, "iota_row", [P, GB * P])
        iota_col = sb(ctx, "iota_col", [P, 1])
        ident = sb(ctx, "ident", [P, P])
        count_d = sb(ctx, "count_d", [P, NB])
        count_s = sb(ctx, "count_s", [P, NB])
        node_end = sb(ctx, "node_end", [P, NB], I32)
        valid = sb(ctx, "valid", [P, NB])
        key = sb(ctx, "key", [P, 1])
        tail = sb(ctx, "tail", [P, RW])

        with ExitStack() as c1:
            SLOTS = 4
            POOL_DUP, ACT_DUP = 8, 8
            w_all = sb(c1, "w_all", [P, R, D])
            rows = sb(c1, "rows", [P, SLOTS, R, 2 * D])
            xb = sb(c1, "xb", [P, 2, D])
            xbT = sb(c1, "xbT", [P, SLOTS, P])
            ps_x = [ps(c1, f"ps_x{k}", [P, P]) for k in range(2)]
            QUART = R * D // 4
            ps_p = [ps(c1, f"ps_p{k}", [P, QUART]) for k in range(4)]
            x_in, x_zero, w_zero = sem(c1, "x_in"), sem(c1, "x_zero"), sem(c1, "w_zero")
            w_in, idx_in, idx_pad = sem(c1, "w_in"), sem(c1, "idx_in"), sem(c1, "idx_pad")
            iota_done, const_done = sem(c1, "iota_done"), sem(c1, "const_done")
            xb_ready, xT_ready, xbT_ready = sem(c1, "xb_ready"), sem(c1, "xT_ready"), sem(c1, "xbT_ready")
            proj_ready = [sem(c1, f"proj_ready{k}") for k in range(4)]
            taken = [sem(c1, f"taken{k}") for k in range(4)]
            dup_ready = sem(c1, "dup_ready")
            stored = [sem(c1, f"stored{s}") for s in range(SLOTS)]
            pool_past, pe_past = sem(ctx, "pool_past"), sem(c1, "pe_past")

            def each_block(engine, step):
                for b in range(SLOTS):
                    step(b, b, 0)
                with engine.Fori(1, NB // SLOTS) as i:
                    for s in range(SLOTS):
                        step(SLOTS * i + s, s, i)
                for b in range(NB // SLOTS * SLOTS, NB):
                    step(b, b % SLOTS, b // SLOTS)

            with nc.Block() as block:
                @block.sync
                def _(sp):
                    sp.wait_ge(x_zero, 1)
                    sp.dma_start(xs[:, 0:NB - 1, :], x[0:(NB - 1) * P, :].rearrange("(b j) d -> j b d", j=P)).then_inc(x_in, 16)
                    sp.dma_start(xs[0:TAILROWS, NB - 1, :], x[(NB - 1) * P:N, :]).then_inc(x_in, 16)
                    sp.dma_start(w_all[0:D, :, :], rel_w.rearrange("r d e -> d r e")).then_inc(w_in, 16)
                    sp.wait_ge(idx_pad, 4)
                    sp.dma_start(src_sb[:, 0:T], src.rearrange("(p t) -> p t", p=P)).then_inc(idx_in, 16)
                    sp.dma_start(dst_sb[:, 1:1 + T], dst.rearrange("(p t) -> p t", p=P)).then_inc(idx_in, 16)
                    with nc.allow_non_contiguous_dma(reason="one number of each partition"):
                        sp.dma_start(head_next[0:P - 1, :], dst[T:E].rearrange("(p t) -> p t", p=P - 1)[:, 0:1]).then_inc(idx_in, 16)

                    def store(b, s, i):
                        sp.wait_ge(dup_ready, b + 1)
                        for k in range(4):
                            sp.wait_ge(taken[k], b + 1)
                        sp.dma_start(table[bass.ds(b * P * R, P * R), :].rearrange("(j r) c -> j (r c)", r=R),
                                     rows[:, s, :, :].rearrange("p r c -> p (r c)")).then_inc(stored[s], 16)

                    each_block(sp, store)
                    for s in range(SLOTS):
                        sp.wait_ge(stored[s], 16 * len(range(s, NB, SLOTS)))
                    sp.wait_ge(idx_in, 48)

                @block.gpsimd
                def _(pool):
                    pool.iota(iota_row[:, :], [[1, GB * P]], base=0, channel_multiplier=0,
                              allow_small_or_imprecise_dtypes=True).then_inc(iota_done, 1)
                    pool.iota(iota_col[:, :], [[0, 1]], base=0, channel_multiplier=1,
                              allow_small_or_imprecise_dtypes=True).then_inc(iota_done, 1)
                    pool.wait_ge(x_in, 32)

                    def duplicate(b, s, i):
                        if later(b):
                            pool.wait_ge(xbT_ready, b)
                        pool.sem_inc(pool_past, 1)
                        pool.tensor_copy(xb[:, :, :], xs[:, bass.ds(b, 1), :].to_broadcast([P, 2, D])).then_inc(xb_ready, 1)
                        if later(i):
                            pool.wait_ge(stored[s], 16 * i)
                        pool.sem_inc(pool_past, 1)
                        pool.tensor_copy(rows[:, s, R - POOL_DUP:R, D:2 * D],
                                         xs[:, bass.ds(b, 1), :].to_broadcast([P, POOL_DUP, D])).then_inc(dup_ready, 1)

                    each_block(pool, duplicate)

                @block.tensor
                def _(pe):
                    pe.wait_ge(const_done, 1)
                    pe.wait_ge(w_zero, 1)
                    pe.wait_ge(w_in, 16)

                    def transpose_x(b, k):
                        pe.wait_ge(xb_ready, b + 1)
                        pe.sem_inc(pe_past, 1)
                        nc.tensor.transpose(ps_x[k][:, :], xb[:, :, :].rearrange("p a d -> p (a d)"), ident[:, :]).then_inc(xT_ready, 1)

                    def project(b, s, i):
                        if not (isinstance(b, int) and b == NB - 1):
                            transpose_x(b + 1, (s + 1) % 2)
                        pe.wait_ge(xbT_ready, b + 1)
                        for k in range(4):
                            if later(b):
                                pe.wait_ge(taken[k], b)
                            nc.tensor.matmul(ps_p[k][:, :], xbT[:, s, :],
                                             w_all[:, k * R // 4:(k + 1) * R // 4, :].rearrange("d r e -> d (r e)"),
                                             start=True, stop=True).then_inc(proj_ready[k], 1)

                    transpose_x(0, 0)
                    each_block(pe, project)

                def take_out(engine, copy, k, b, s, i):
                    engine.wait_ge(proj_ready[k], b + 1)
                    if later(i):
                        engine.wait_ge(stored[s], 16 * i)
                    copy(rows[:, s, k * R // 4:(k + 1) * R // 4, 0:D],
                         ps_p[k][:, :].rearrange("p (r e) -> p r e", e=D)).then_inc(taken[k], 1)

                @block.vector
                def _(dve):
                    nc.vector.memset(xs[:, NB - 1, :], 0.0).then_inc(x_zero, 1)
                    nc.vector.memset(w_all[D:P, :, :], 0.0).then_inc(w_zero, 1)
                    nc.vector.memset(src_sb[:, T:], 0).then_inc(idx_pad, 1)
                    nc.vector.memset(dst_sb[:, 0:1], -1).then_inc(idx_pad, 1)
                    nc.vector.memset(dst_sb[:, 1 + T:], 0).then_inc(idx_pad, 1)
                    nc.vector.memset(head_next[:, :], -1).then_inc(idx_pad, 1)
                    dve.wait_ge(x_in, 32)
                    dve.wait_ge(iota_done, 2)
                    nc.vector.tensor_scalar(ident[:, :], iota_row[:, 0:P], iota_col[:, 0:1], None, ALU.is_equal).then_inc(const_done, 1)

                    def quarters(b, s, i):
                        take_out(dve, nc.vector.tensor_copy, 0, b, s, i)
                        nc.vector.tensor_copy(rows[:, s, 0:R - POOL_DUP - ACT_DUP, D:2 * D],
                                              xs[:, bass.ds(b, 1), :].to_broadcast([P, R - POOL_DUP - ACT_DUP, D]))
                        take_out(dve, nc.vector.tensor_copy, 2, b, s, i)

                    each_block(dve, quarters)

                @block.scalar
                def _(act):
                    act.wait_ge(x_in, 32)

                    def take_x(b, k, s):
                        act.wait_ge(xT_ready, b + 1)
                        nc.scalar.copy(xbT[:, s, :], ps_x[k][:, :]).then_inc(xbT_ready, 1)

                    def quarters(b, s, i):
                        if not (isinstance(b, int) and b == NB - 1):
                            take_x(b + 1, (s + 1) % 2, (s + 1) % SLOTS)
                        take_out(act, nc.scalar.copy, 1, b, s, i)
                        nc.scalar.copy(rows[:, s, R - POOL_DUP - ACT_DUP:R - POOL_DUP, D:2 * D],
                                       xs[:, bass.ds(b, 1), :].to_broadcast([P, ACT_DUP, D]))
                        take_out(act, nc.scalar.copy, 3, b, s, i)

                    take_x(0, 0, 0)
                    each_block(act, quarters)

        with ExitStack() as c2:
            type_sb = sb(c2, "type_sb", [P, T + 2 * G], I32)
            idx_s = sb(c2, "idx_s", [P, 2, G], I32)
            idx_d = sb(c2, "idx_d", [P, 2, G], I32)
            gs = sb(c2, "gs", [P, 2, G, 2 * D])
            gd = sb(c2, "gd", [P, 2, G, D])
            ef = sb(c2, "ef", [P, 2, G, D])
            att = sb(c2, "att", [P, G])
            same = sb(c2, "same", [P, G])
            gap = sb(c2, "gap", [P, G])
            mx = sb(c2, "mx", [P, 1 + G])
            ex_in = sb(c2, "ex_in", [P, 2, G])
            ex = sb(c2, "ex", [P, 2, G])
            keep = sb(c2, "keep", [P, W, 1 + G])
            add = sb(c2, "add", [P, W, 1 + G])
            run = sb(c2, "run", [P, W, 1 + G])
            rowbuf = sb(c2, "rowbuf", [P, 2, G, RW])
            digit = sb(c2, "digit", [P, 4, G], I32)
            lo_s = sb(c2, "lo_s", [P, G, P], BF16)
            lo_d = sb(c2, "lo_d", [P, G, P], BF16)
            hi_s = sb(c2, "hi_s", [P, G, NB], BF16)
            hi_d = sb(c2, "hi_d", [P, G, NB], BF16)
            zero = sb(c2, "zero", [P, P], BF16)
            hist_s, hist_d = ps(c2, "hist_s", [P, NB]), ps(c2, "hist_d", [P, NB])
            type_in, type_pad = sem(c2, "type_in"), sem(c2, "type_pad")
            ef_in = [sem(c2, f"ef_in{s}") for s in range(2)]
            gs_in = [sem(c2, f"gs_in{s}") for s in range(2)]
            gd_in = [sem(c2, f"gd_in{s}") for s in range(2)]
            stored = [sem(c2, f"rows_stored{s}") for s in range(2)]
            vstep = sem(c2, "vstep")
            slot_ready = sem(c2, "slot_ready")
            tanh_arg, tanh_done = sem(c2, "tanh_arg"), sem(c2, "tanh_done")
            exp_arg, exp_done = sem(c2, "exp_arg"), sem(c2, "exp_done")
            keep_ready, run_ready, rows_ready = sem(c2, "keep_ready"), sem(c2, "run_ready"), sem(c2, "rows_ready")
            onehot_ready, onehot_used = sem(c2, "onehot_ready"), sem(c2, "onehot_used")
            hist_begun, hist_done, init_done = sem(c2, "hist_begun"), sem(c2, "hist_done"), sem(c2, "init_done")
            edges = edge_attr.rearrange("(p t) d -> p t d", p=P)
            sums0_v = sums0.rearrange("(p t) w -> p t w", p=P)

            with nc.Block() as block:
                @block.sync
                def _(sp):
                    sp.wait_ge(type_pad, 1)
                    sp.dma_start(type_sb[:, 0:T], etype.rearrange("(p t) -> p t", p=P)).then_inc(type_in, 16)

                    def load(c, s):
                        sp.dma_start(ef[:, s, :, :], edges[:, bass.ds(c * G, G), :]).then_inc(ef_in[s], 16)

                    load(0, 0)
                    load(1, 1)
                    with sp.Fori(0, PAIRS - 1) as i:
                        sp.wait_ge(tanh_arg, 2 * i + 1)
                        load(2 * i + 2, 0)
                        sp.wait_ge(tanh_arg, 2 * i + 2)
                        load(2 * i + 3, 1)
                    sp.wait_ge(tanh_arg, CHUNKS - 2)
                    load(CHUNKS - 1, 0)

                @block.gpsimd
                def _(pool):
                    def gather(c, s):
                        pool.wait_ge(slot_ready, c + 1)
                        pool.sem_inc(pool_past, 1)
                        for g in range(G):
                            pool.indirect_dma_start(
                                out=gs[:, s, g, :], out_offset=None, in_=table,
                                in_offset=bass.IndirectOffsetOnAxis(ap=idx_s[:, s, g:g + 1], axis=0)).then_inc(gs_in[s], 16)
                            pool.indirect_dma_start(
                                out=gd[:, s, g, :], out_offset=None, in_=table_half,
                                in_offset=bass.IndirectOffsetOnAxis(ap=idx_d[:, s, g:g + 1], axis=0)).then_inc(gd_in[s], 16)

                    with pool.Fori(0, PAIRS) as i:
                        gather(2 * i, 0)
                        gather(2 * i + 1, 1)
                    gather(CHUNKS - 1, 0)

                @block.vector
                def _(dve):
                    link = Steps(dve, vstep)
                    SETUP, PER_CHUNK = 6, 13

                    def stage(c, s):
                        at = bass.ds(c * G, G)
                        at_d = bass.ds(c * G + 1, G)
                        nc.vector.scalar_tensor_tensor(out=idx_s[:, s, :], in0=src_sb[:, at], scalar=float(R),
                                                       in1=type_sb[:, at], op0=ALU.mult, op1=ALU.add)
                        link.then(nc.vector.scalar_tensor_tensor(out=idx_d[:, s, :], in0=dst_sb[:, at_d], scalar=float(R),
                                                                 in1=type_sb[:, at], op0=ALU.mult, op1=ALU.add))
                        nc.vector.tensor_scalar(idx_d[:, s, :], idx_d[:, s, :], 2.0, None, ALU.mult).then_inc(slot_ready, 1)

                    nc.vector.memset(type_sb[:, T:], 0).then_inc(type_pad, 1)
                    nc.vector.memset(zero[:, :], 0.0).then_inc(init_done, 1)
                    link.then(nc.vector.memset(digit[:, :, :], 0))
                    link.then(nc.vector.memset(mx[:, :], -BIG))
                    link.then(nc.vector.memset(keep[:, :, :], 0.0))
                    link.then(nc.vector.memset(run[:, :, :], 0.0))
                    nc.vector.memset(add[:, :, :], 0.0).then_inc(init_done, 1)
                    dve.wait_ge(type_in, 16)
                    stage(0, 0)
                    stage(1, 1)
                    assert link.n == SETUP

                    def chunk(c, s, i):
                        link.at(SETUP + c * PER_CHUNK)
                        at = bass.ds(c * G, G)
                        at_d = bass.ds(c * G + 1, G)
                        dve.wait_ge(ef_in[s], 16 * (i + 1))
                        dve.wait_ge(gd_in[s], 16 * G * (i + 1))
                        nc.vector.tensor_tensor(gd[:, s, :, :], gd[:, s, :, :], ef[:, s, :, :], ALU.add).then_inc(tanh_arg, 1)
                        nc.vector.tensor_scalar(digit[:, 0, :], src_sb[:, at], 127, None, ALU.bitwise_and)
                        nc.vector.tensor_scalar(digit[:, 1, :], src_sb[:, at], 7, None, ALU.logical_shift_right)
                        nc.vector.tensor_scalar(digit[:, 2, :], dst_sb[:, at_d], 127, None, ALU.bitwise_and)
                        link.then(nc.vector.tensor_scalar(digit[:, 3, :], dst_sb[:, at_d], 7, None, ALU.logical_shift_right))
                        if later(c):
                            dve.wait_ge(onehot_used, c)
                        for k, (hot, width) in enumerate(((lo_s, P), (hi_s, NB), (lo_d, P), (hi_d, NB))):
                            last = nc.vector.tensor_tensor(
                                hot[:, :, :], iota_row[:, 0:width].unsqueeze(1).to_broadcast([P, G, width]),
                                digit[:, k, :].unsqueeze(2).to_broadcast([P, G, width]), ALU.is_equal)
                        last.then_inc(onehot_ready, 1)
                        link.then(nc.vector.tensor_tensor(same[:, :], dst_sb[:, at_d], dst_sb[:, at], ALU.is_equal))
                        link.then(nc.vector.tensor_scalar(gap[:, :], same[:, :], -1.0, BIG, ALU.add, ALU.mult))
                        dve.wait_ge(gs_in[s], 16 * G * (i + 1))
                        dve.wait_ge(tanh_done, c + 1)
                        link.then(nc.vector.tensor_tensor(gd[:, s, :, :], gd[:, s, :, :], gs[:, s, :, 0:D], ALU.mult))
                        link.then(nc.vector.tensor_reduce(att[:, :], gd[:, s, :, :], AX.X, ALU.add))
                        if later(c):
                            dve.wait_ge(rows_ready, c)
                        link.then(nc.vector.tensor_copy(mx[:, 0:1], mx[:, G:G + 1]))
                        link.then(nc.vector.tensor_tensor_scan(mx[:, 1:], gap[:, :], att[:, :], mx[:, 0:1], ALU.add, ALU.max))
                        link.then(nc.vector.tensor_tensor(ex_in[:, 0, :], att[:, :], mx[:, 1:], ALU.subtract))
                        link.then(nc.vector.tensor_tensor(ex_in[:, 1, :], mx[:, 0:G], gap[:, :], ALU.add))
                        nc.vector.tensor_tensor(ex_in[:, 1, :], ex_in[:, 1, :], mx[:, 1:], ALU.subtract).then_inc(exp_arg, 1)
                        link.then(nc.vector.tensor_copy(add[:, :, 0], run[:, :, G]))
                        dve.wait_ge(exp_done, c + 1)
                        link.then(nc.vector.tensor_copy(add[:, D, 1:], ex[:, 0, :]))
                        link.then(nc.vector.tensor_tensor(
                            add[:, 0:D, 1:].rearrange("p d t -> p t d"), gs[:, s, :, D:2 * D],
                            ex[:, 0, :].unsqueeze(2).to_broadcast([P, G, D]), ALU.mult))
                        dve.wait_ge(keep_ready, c + 1)
                        nc.vector.tensor_tensor_scan(run[:, :, :].rearrange("p w t -> p (w t)"),
                                                     keep[:, :, :].rearrange("p w t -> p (w t)"),
                                                     add[:, :, :].rearrange("p w t -> p (w t)"),
                                                     0.0, ALU.mult, ALU.add).then_inc(run_ready, 1)
                        stage(c + 2, s)
                        assert link.n == PER_CHUNK, link.n

                    chunk(0, 0, 0)
                    chunk(1, 1, 0)
                    with dve.Fori(1, PAIRS) as i:
                        chunk(2 * i, 0, i)
                        chunk(2 * i + 1, 1, i)
                    chunk(CHUNKS - 1, 0, PAIRS)
                    dve.wait_ge(hist_done, 1)
                    nc.vector.tensor_copy(count_s[:, :], hist_s[:, :])
                    nc.vector.tensor_copy(count_d[:, :], hist_d[:, :])
                    nc.vector.tensor_copy(tail[:, 0:W], run[:, :, G])
                    nc.vector.tensor_copy(tail[:, W:RW], mx[:, G:G + 1])

                @block.scalar
                def _(act):
                    act.wait_ge(init_done, 2)

                    def chunk(c, s, i):
                        act.wait_ge(tanh_arg, c + 1)
                        nc.scalar.activation(gd[:, s, :, :], gd[:, s, :, :], ACT.Tanh).then_inc(tanh_done, 1)
                        act.wait_ge(exp_arg, c + 1)
                        nc.scalar.activation(ex[:, :, :], ex_in[:, :, :], ACT.Exp).then_inc(exp_done, 1)
                        act.wait_ge(exp_done, c + 1)
                        nc.scalar.copy(keep[:, :, 1:], ex[:, 1, :].unsqueeze(1).to_broadcast([P, W, G])).then_inc(keep_ready, 1)
                        act.wait_ge(run_ready, c + 1)
                        if later(i):
                            act.wait_ge(stored[s], 16 * i)
                        nc.scalar.copy(rowbuf[:, s, :, 0:W], run[:, :, 1:].rearrange("p w t -> p t w"))
                        nc.scalar.copy(rowbuf[:, s, :, W], mx[:, 1:]).then_inc(rows_ready, 1)
                        act.wait_ge(rows_ready, c + 1)
                        act.dma_start(sums0_v[:, bass.ds(c * G, G), :], rowbuf[:, s, :, :]).then_inc(stored[s], 16)

                    chunk(0, 0, 0)
                    chunk(1, 1, 0)
                    with act.Fori(1, PAIRS) as i:
                        chunk(2 * i, 0, i)
                        chunk(2 * i + 1, 1, i)
                    chunk(CHUNKS - 1, 0, PAIRS)
                    act.wait_ge(stored[0], 16 * (PAIRS + 1))
                    act.wait_ge(stored[1], 16 * PAIRS)

                @block.tensor
                def _(pe):
                    pe.wait_ge(init_done, 1)
                    nc.tensor.matmul(hist_s[:, :], zero[:, :], zero[:, 0:NB], start=True, stop=False)
                    nc.tensor.matmul(hist_d[:, :], zero[:, :], zero[:, 0:NB], start=True, stop=False)
                    with pe.Fori(0, CHUNKS) as c:
                        pe.wait_ge(onehot_ready, c + 1)
                        for g in range(G):
                            nc.tensor.matmul(hist_s[:, :], lo_s[:, g, :], hi_s[:, g, :], start=False, stop=False)
                            last = nc.tensor.matmul(hist_d[:, :], lo_d[:, g, :], hi_d[:, g, :], start=False, stop=False)
                        last.then_inc(onehot_used, 1)
                    nc.tensor.matmul(hist_s[:, :], zero[:, :], zero[:, 0:NB], start=False, stop=True)
                    nc.tensor.matmul(hist_d[:, :], zero[:, :], zero[:, 0:NB], start=False, stop=True).then_inc(hist_done, 1)

        tail_stage(nc, sb, ps, sem, dst_sb, head_next, iota_row, iota_col, ident, count_d, count_s,
                   node_end, valid, key, tail)
        attention_nodes(nc, sb, ps, sem, res_w1, res_w2, xs, ident, iota_row, pool_past, node_end, valid, key, tail,
                        count_s, sums0, ytab)

        with ExitStack() as c4:
            idx = sb(c4, "idx", [P, 2, G], I32)
            gy = sb(c4, "gy", [P, 2, G, D])
            same = sb(c4, "same1", [P, G])
            keep = sb(c4, "keep1", [P, D, 1 + G])
            add = sb(c4, "add1", [P, D, 1 + G])
            run = sb(c4, "run1", [P, D, 1 + G])
            rowbuf = sb(c4, "rowbuf1", [P, 2, G, D])
            gy_in = [sem(c4, f"gy_in{s}") for s in range(2)]
            stored = [sem(c4, f"rows1_stored{s}") for s in range(2)]
            slot_ready, same_ready = sem(c4, "slot1_ready"), sem(c4, "same_ready")
            keep_ready, run_ready = sem(c4, "keep1_ready"), sem(c4, "run1_ready")
            rows_ready, init_done, vstep = sem(c4, "rows1_ready"), sem(c4, "init1_done"), sem(c4, "vstep1")
            sums1_v = sums1.rearrange("(p t) w -> p t w", p=P)

            with nc.Block() as block:
                @block.gpsimd
                def _(pool):
                    def gather(c, s):
                        pool.wait_ge(slot_ready, c + 1)
                        pool.sem_inc(pool_past, 1)
                        for g in range(G):
                            pool.indirect_dma_start(
                                out=gy[:, s, g, :], out_offset=None, in_=ytab,
                                in_offset=bass.IndirectOffsetOnAxis(ap=idx[:, s, g:g + 1], axis=0)).then_inc(gy_in[s], 16)

                    with pool.Fori(0, PAIRS) as i:
                        gather(2 * i, 0)
                        gather(2 * i + 1, 1)
                    gather(CHUNKS - 1, 0)

                @block.vector
                def _(dve):
                    link = Steps(dve, vstep)

                    def stage(c, s):
                        nc.vector.tensor_copy(idx[:, s, :], src_sb[:, bass.ds(c * G, G)]).then_inc(slot_ready, 1)

                    nc.vector.memset(keep[:, :, :], 0.0).then_inc(init_done, 1)
                    nc.vector.memset(add[:, :, :], 0.0).then_inc(init_done, 1)
                    link.then(nc.vector.memset(run[:, :, :], 0.0))
                    stage(0, 0)
                    stage(1, 1)

                    def chunk(c, s, i):
                        link.at(1 + c)
                        if later(c):
                            dve.wait_ge(keep_ready, c)
                        nc.vector.tensor_tensor(same[:, :], dst_sb[:, bass.ds(c * G + 1, G)], dst_sb[:, bass.ds(c * G, G)],
                                                ALU.is_equal).then_inc(same_ready, 1)
                        if later(c):
                            dve.wait_ge(rows_ready, c)
                        link.then(nc.vector.tensor_copy(add[:, :, 0], run[:, :, G]))
                        dve.wait_ge(gy_in[s], 16 * G * (i + 1))
                        dve.wait_ge(keep_ready, c + 1)
                        nc.vector.tensor_tensor_scan(run[:, :, :].rearrange("p w t -> p (w t)"),
                                                     keep[:, :, :].rearrange("p w t -> p (w t)"),
                                                     add[:, :, :].rearrange("p w t -> p (w t)"),
                                                     0.0, ALU.mult, ALU.add).then_inc(run_ready, 1)
                        stage(c + 2, s)

                    chunk(0, 0, 0)
                    chunk(1, 1, 0)
                    with dve.Fori(1, PAIRS) as i:
                        chunk(2 * i, 0, i)
                        chunk(2 * i + 1, 1, i)
                    chunk(CHUNKS - 1, 0, PAIRS)
                    dve.wait_ge(run_ready, CHUNKS)
                    nc.vector.tensor_copy(tail[:, 0:D], run[:, :, G])

                @block.scalar
                def _(act):
                    act.wait_ge(init_done, 2)

                    def chunk(c, s, i):
                        act.wait_ge(gy_in[s], 16 * G * (i + 1))
                        nc.scalar.copy(add[:, :, 1:].rearrange("p d t -> p t d"), gy[:, s, :, :])
                        act.wait_ge(same_ready, c + 1)
                        nc.scalar.copy(keep[:, :, 1:], same[:, :].unsqueeze(1).to_broadcast([P, D, G])).then_inc(keep_ready, 1)
                        act.wait_ge(run_ready, c + 1)
                        if later(i):
                            act.wait_ge(stored[s], 16 * i)
                        nc.scalar.copy(rowbuf[:, s, :, :], run[:, :, 1:].rearrange("p w t -> p t w")).then_inc(rows_ready, 1)
                        act.wait_ge(rows_ready, c + 1)
                        act.dma_start(sums1_v[:, bass.ds(c * G, G), :], rowbuf[:, s, :, :]).then_inc(stored[s], 16)

                    chunk(0, 0, 0)
                    chunk(1, 1, 0)
                    with act.Fori(1, PAIRS) as i:
                        chunk(2 * i, 0, i)
                        chunk(2 * i + 1, 1, i)
                    chunk(CHUNKS - 1, 0, PAIRS)
                    act.wait_ge(stored[0], 16 * (PAIRS + 1))
                    act.wait_ge(stored[1], 16 * PAIRS)

        mean_nodes(nc, sb, ps, sem, xs, iota_row, pool_past, node_end, valid, key, tail, count_d, sums1, out)


_INS = ['x', 'src', 'dst', 'edge_attr_64', 'edge_type_32', 'L0_gnn_relation_weight', 'L0_gnn_res_w1', 'L0_gnn_res_w2']
_OUTS = [((N, D), 'float32')]


def kernel(**inputs):
    import numpy as _np
    import concourse.bacc as _bacc
    from concourse import mybir as _mybir
    from concourse.bass_utils import run_bass_kernel_spmd as _run

    nc = _bacc.Bacc("TRN2", target_bir_lowering=False, num_devices=1)
    arrays, args = {}, []
    for name in _INS:
        a = _np.ascontiguousarray(inputs[name])
        arrays[f"in_{name}_dram"] = a
        args.append(nc.dram_tensor(f"in_{name}_dram", a.shape, _mybir.dt.from_np(a.dtype), kind="ExternalInput").ap())
    for i, (shape, dtype) in enumerate(_OUTS):
        dt = _mybir.dt.from_np(_np.dtype(dtype))
        args.append(nc.dram_tensor(f"out_{i}_dram", shape, dt, kind="ExternalOutput").ap())
    gnn_program(nc, *args)
    r = _run(nc, [arrays], core_ids=[0])
    return r.results[0]["out_0_dram"]
```

```python
import concourse.bass as bass
from concourse import mybir
from contextlib import ExitStack

F32 = mybir.dt.float32
BF16 = mybir.dt.bfloat16
I32 = mybir.dt.int32
ALU = mybir.AluOpType
ACT = mybir.ActivationFunctionType
AX = mybir.AxisListType

P = 128
N, E, D, R = 12500, 400000, 64, 32
T = E // P
G = 25
CHUNKS = T // G
PAIRS = CHUNKS // 2
NB = -(-N // P)
NPAD = NB * P
TAILROWS = N - (NB - 1) * P
GB = 7
GROUPS = NB // GB
PB = 2 * GB
W = D + 1
RW = D + 2
BIG = 1.0e30
EPS = 1.0e-5
SLOPE = 0.01
assert T * P == E and G * CHUNKS == T and GB * GROUPS == NB and GROUPS % 2 == 0


def later(count):
    return not (isinstance(count, int) and count == 0)


class Steps:

    def __init__(self, engine, sem):
        self.engine, self.sem, self.base, self.n = engine, sem, 0, 0

    def at(self, base):
        self.base, self.n = base, 0

    def then(self, instruction):
        self.n += 1
        instruction.then_inc(self.sem, 1)
        self.engine.wait_ge(self.sem, self.base + self.n)


def tail_stage(nc, sb, ps, sem, dst_sb, head_next, iota_row, iota_col, ident, count_d, count_s,
               node_end, valid, key, tail):
    with ExitStack() as c:
        upto = sb(c, "upto", [P, P])
        after = sb(c, "after", [P, P])
        ones = sb(c, "ones", [P, P])
        wide = sb(c, "wide", [P, 2, P])
        group = sb(c, "group", [P, P])
        work = sb(c, "work", [P, P])
        total = sb(c, "total", [P, NB])
        before = sb(c, "before", [P, NB])
        goes_on = sb(c, "goes_on", [P, 1])
        small = sb(c, "small", [P, 4])
        ps_in = ps(c, "ps_in", [P, NB])
        ps_all = ps(c, "ps_all", [P, NB])
        ps_wide = ps(c, "ps_wide", [P, 2, P])
        vstep, ready, mm, ex_arg, ex_done = (sem(c, n) for n in ("vstep_t", "ready_t", "mm_t", "exarg_t", "exdone_t"))

        with nc.Block() as block:
            @block.vector
            def _(dve):
                link = Steps(dve, vstep)
                link.then(nc.vector.memset(ones[:, :], 1.0))
                link.then(nc.vector.tensor_scalar(upto[:, :], iota_row[:, 0:P], iota_col[:, 0:1], None, ALU.is_ge))
                link.then(nc.vector.tensor_scalar(after[:, :], iota_row[:, 0:P], iota_col[:, 0:1], None, ALU.is_gt))
                link.then(nc.vector.tensor_tensor(goes_on[:, :], dst_sb[:, T:T + 1], head_next[:, :], ALU.is_equal))
                link.then(nc.vector.tensor_scalar(small[:, 0:1], dst_sb[:, T:T + 1], 5.0, None, ALU.add))
                link.then(nc.vector.tensor_tensor(small[:, 1:2], small[:, 0:1], goes_on[:, :], ALU.mult))
                link.then(nc.vector.tensor_scalar(key[:, :], small[:, 1:2], -5.0, None, ALU.add))
                link.then(nc.vector.tensor_copy(wide[:, 0, :], key[:, 0:1].to_broadcast([P, P])))
                nc.vector.tensor_copy(wide[:, 1, :], tail[:, W:RW].to_broadcast([P, P])).then_inc(ready, 1)
                dve.wait_ge(mm, 1)
                link.then(nc.vector.tensor_copy(total[:, :], ps_all[:, :]))
                link.then(nc.vector.tensor_tensor_scan(before[:, :], ones[:, 0:NB], total[:, :], 0.0, ALU.mult, ALU.add))
                link.then(nc.vector.tensor_tensor(before[:, :], before[:, :], total[:, :], ALU.subtract))
                link.then(nc.vector.tensor_tensor(before[:, :], before[:, :], ps_in[:, :], ALU.add))
                link.then(nc.vector.tensor_scalar(node_end[:, :], before[:, :], -1.0, 0.0, ALU.add, ALU.max))
                link.then(nc.vector.tensor_scalar(valid[:, :], count_d[:, :], 1.0, None, ALU.min))
                link.then(nc.vector.tensor_scalar(count_d[:, :], count_d[:, :], 1.0, None, ALU.max))
                link.then(nc.vector.tensor_scalar(count_s[:, :], count_s[:, :], 1.0, None, ALU.max))
                link.then(nc.vector.reciprocal(count_d[:, :], count_d[:, :]))
                link.then(nc.vector.reciprocal(count_s[:, :], count_s[:, :]))
                link.then(nc.vector.tensor_scalar(group[:, :], ps_wide[:, 0, :], key[:, 0:1], None, ALU.is_equal))
                link.then(nc.vector.tensor_scalar(work[:, :], group[:, :], -1.0, BIG, ALU.add, ALU.mult))
                link.then(nc.vector.tensor_tensor(work[:, :], work[:, :], ps_wide[:, 1, :], ALU.add))
                link.then(nc.vector.tensor_reduce(small[:, 2:3], work[:, :], AX.X, ALU.max))
                nc.vector.tensor_tensor(small[:, 3:4], tail[:, W:RW], small[:, 2:3], ALU.subtract).then_inc(ex_arg, 1)
                link.then(nc.vector.tensor_tensor(work[:, :], group[:, :], after[:, :], ALU.mult))
                link.then(nc.vector.tensor_reduce(small[:, 0:1], work[:, :], AX.X, ALU.max))
                link.then(nc.vector.tensor_scalar(small[:, 0:1], small[:, 0:1], -1.0, 1.0, ALU.mult, ALU.add))
                link.then(nc.vector.tensor_tensor(tail[:, W:RW], small[:, 2:3], small[:, 0:1], ALU.mult))
                dve.wait_ge(ex_done, 1)
                link.then(nc.vector.tensor_scalar(tail[:, 0:W], tail[:, 0:W], small[:, 1:2], None, ALU.mult))

            @block.scalar
            def _(act):
                act.wait_ge(ex_arg, 1)
                nc.scalar.activation(small[:, 1:2], small[:, 3:4], ACT.Exp).then_inc(ex_done, 1)

            @block.tensor
            def _(pe):
                pe.wait_ge(ready, 1)
                nc.tensor.matmul(ps_in[:, :], upto[:, :], count_d[:, :], start=True, stop=True)
                nc.tensor.matmul(ps_all[:, :], ones[:, :], count_d[:, :], start=True, stop=True)
                nc.tensor.matmul(ps_wide[:, 0, :], wide[:, 0, :], ident[:, :], start=True, stop=True)
                nc.tensor.matmul(ps_wide[:, 1, :], wide[:, 1, :], ident[:, :], start=True, stop=True).then_inc(mm, 1)


def node_gathers(pool, pool_past, link_sem, idx, rows, rows_in, table):
    def gather(g, s):
        pool.wait_ge(link_sem, g + 1)
        pool.sem_inc(pool_past, 1)
        for b in range(GB):
            pool.indirect_dma_start(out=rows[:, s, b, :], out_offset=None, in_=table,
                                    in_offset=bass.IndirectOffsetOnAxis(ap=idx[:, s, b:b + 1], axis=0)).then_inc(rows_in[s], 16)

    with pool.Fori(0, GROUPS // 2) as i:
        gather(2 * i, 0)
        gather(2 * i + 1, 1)


def wide_of(v, n=D):
    return v.unsqueeze(2).to_broadcast([P, v.shape[1], n])


def attention_nodes(nc, sb, ps, sem, res_w1, res_w2, xs, ident, iota_row, pool_past, node_end, valid, key, tail,
                    count_s, sums0, ytab):
    with ExitStack() as c:
        idx = sb(c, "idx_n", [P, 2, GB], I32)
        landed = sb(c, "landed_n", [P, 2, GB, RW])
        rows = sb(c, "rows_n", [P, PB, RW])
        mask = sb(c, "mask_n", [P, PB * P])
        shifted = sb(c, "shifted_n", [P, 1])
        carry = sb(c, "carry_n", [P, PB, RW])
        carry_max = sb(c, "carry_max", [P, PB])
        no_edge = sb(c, "no_edge", [P, NB])
        ex_in = sb(c, "ex_in_n", [P, 2, PB])
        ex = sb(c, "ex_n", [P, 2, PB])
        most = sb(c, "most", [P, PB])
        den = sb(c, "den", [P, PB])
        hnb = sb(c, "hnb", [P, PB, D])
        both = sb(c, "both", [P, PB, 2, D])
        bothT = sb(c, "bothT", [P, 2, GB, P])
        part = sb(c, "part", [P, 2, PB, D])
        z = sb(c, "z", [P, PB, D])
        sq = sb(c, "sq", [P, PB, D])
        stat = sb(c, "stat", [P, 4, PB])
        y = sb(c, "y", [P, 2, PB, D])
        eps = sb(c, "eps", [P, 1])
        w_raw = sb(c, "w_raw", [D, 2, D])
        wT = sb(c, "wT", [P, D])
        BANK = 512
        ps_c = ps(c, "ps_c", [P, 2, BANK])
        ps_t = [ps(c, f"ps_t{k}", [P, 4, P]) for k in range(2)]
        ps_o = [ps(c, f"ps_o{k}", [P, 2, BANK]) for k in range(2)]
        ps_w = ps_c[:, 0, 0:D]

        def by_group(v):
            return v.rearrange("p (s b) d -> p s b d", s=2)

        def in_banks(v, width):
            return v[:, :, 0:GB * width].rearrange("p s (b d) -> p s b d", d=width)

        rows_in = [sem(c, f"rows_in{s}") for s in range(2)]
        y_out = [sem(c, f"y_out{s}") for s in range(2)]
        rows_ready = sem(c, "rows_ready_n")
        staged, vstep, w_in = sem(c, "staged_n"), sem(c, "vstep_n"), sem(c, "w_in_n")
        mask_ready, carry_mm, carry_ready = sem(c, "mask_ready"), sem(c, "carry_mm"), sem(c, "carry_ready")
        ex_arg, ex_done, eps_ready = sem(c, "ex_arg_n"), sem(c, "ex_done_n"), sem(c, "eps_ready")
        both_ready, both_t, bothT_ready = sem(c, "both_ready"), sem(c, "both_t"), sem(c, "bothT_ready")
        prod, part_ready = sem(c, "prod"), sem(c, "part_ready")
        centred, sq_ready = sem(c, "centred"), sem(c, "sq_ready")
        var_ready, std_ready, y_ready = sem(c, "var_ready"), sem(c, "std_ready"), sem(c, "y_ready")
        w_mm, w_ready = sem(c, "w_mm"), sem(c, "w_ready")

        pairs = GROUPS // 2
        assert pairs % 2 == 1

        with nc.Block() as block:
            @block.sync
            def _(sp):
                sp.dma_start(w_raw[:, 0, :], res_w1).then_inc(w_in, 16)
                sp.dma_start(w_raw[:, 1, :], res_w2).then_inc(w_in, 16)

                def store(i, k):
                    sp.wait_ge(y_ready, i + 1)
                    sp.dma_start(ytab[bass.ds(i * PB * P, PB * P), :].rearrange("(b j) d -> j b d", j=P),
                                 y[:, k, :, :]).then_inc(y_out[k], 16)

                with sp.Fori(0, pairs // 2) as h:
                    store(2 * h, 0)
                    store(2 * h + 1, 1)
                store(pairs - 1, 0)
                sp.wait_ge(y_out[0], 16 * (pairs // 2 + 1))
                sp.wait_ge(y_out[1], 16 * (pairs // 2))

            @block.gpsimd
            def _(pool):
                node_gathers(pool, pool_past, staged, idx, landed, rows_in, sums0)

            @block.vector
            def _(dve):
                link = Steps(dve, vstep)
                SETUP, FRONT, BACK = 3, 11, 7

                def stage(g, s):
                    nc.vector.tensor_copy(idx[:, s, :], node_end[:, bass.ds(g * GB, GB)]).then_inc(staged, 1)

                nc.vector.memset(eps[:, :], EPS).then_inc(eps_ready, 1)
                stage(0, 0)
                stage(1, 1)
                link.then(nc.vector.tensor_scalar(no_edge[:, :], valid[:, :], -1.0, 1.0, ALU.mult, ALU.add))
                link.then(nc.vector.tensor_copy(shifted[:, :], key[:, :]))

                def masks(i):
                    nc.vector.tensor_scalar(mask[:, :], iota_row[:, :], shifted[:, 0:1], None, ALU.is_equal).then_inc(mask_ready, 1)
                    dve.wait_ge(mask_ready, i + 1)
                    link.then(nc.vector.tensor_scalar(shifted[:, :], shifted[:, :], float(-PB * P), None, ALU.add))

                def maxima(i):
                    dve.wait_ge(carry_ready, i + 1)
                    link.then(nc.vector.tensor_scalar(carry_max[:, :], carry[:, :, D], 0.0, None, ALU.is_gt))
                    link.then(nc.vector.tensor_scalar(carry_max[:, :], carry_max[:, :], -1.0, BIG, ALU.add, ALU.mult))
                    link.then(nc.vector.tensor_tensor(carry_max[:, :], carry_max[:, :], carry[:, :, W], ALU.add))
                    dve.wait_ge(rows_ready, 2 * i + 2)
                    link.then(nc.vector.tensor_tensor(most[:, :], carry_max[:, :], rows[:, :, W], ALU.max))
                    nc.vector.tensor_tensor(ex_in[:, 0, :], rows[:, :, W], most[:, :], ALU.subtract)
                    nc.vector.tensor_tensor(ex_in[:, 1, :], carry_max[:, :], most[:, :], ALU.subtract).then_inc(ex_arg, 1)

                def neighbours(i):
                    at = bass.ds(i * PB, PB)
                    dve.wait_ge(ex_done, i + 1)
                    link.then(nc.vector.tensor_tensor(ex[:, 0, :], ex[:, 0, :], valid[:, at], ALU.mult))
                    nc.vector.tensor_tensor(rows[:, :, 0:W], rows[:, :, 0:W], wide_of(ex[:, 0, :], W), ALU.mult)
                    link.then(nc.vector.tensor_tensor(carry[:, :, 0:W], carry[:, :, 0:W], wide_of(ex[:, 1, :], W), ALU.mult))
                    link.then(nc.vector.tensor_tensor(carry[:, :, 0:W], carry[:, :, 0:W], rows[:, :, 0:W], ALU.add))
                    link.then(nc.vector.tensor_tensor(den[:, :], carry[:, :, D], no_edge[:, at], ALU.add))
                    link.then(nc.vector.reciprocal(den[:, :], den[:, :]))
                    link.then(nc.vector.tensor_tensor(hnb[:, :, :], carry[:, :, 0:D], wide_of(den[:, :]), ALU.mult))
                    nc.vector.tensor_tensor(both[:, :, 0, :], xs[:, at, :], hnb[:, :, :], ALU.add)
                    nc.vector.tensor_tensor(both[:, :, 1, :], xs[:, at, :], hnb[:, :, :], ALU.mult).then_inc(both_ready, 1)

                def residual(i):
                    at = bass.ds(i * PB, PB)
                    dve.wait_ge(part_ready, 2 * i + 2)
                    for k in range(2):
                        last_max = nc.vector.tensor_tensor(by_group(part[:, k, :, :]), by_group(part[:, k, :, :]),
                                                           in_banks(ps_o[k], D), ALU.max)
                    link.then(last_max)
                    link.then(nc.vector.tensor_tensor(z[:, :, :], part[:, 0, :, :], part[:, 1, :, :], ALU.add))
                    link.then(nc.vector.tensor_tensor(z[:, :, :], z[:, :, :], xs[:, at, :], ALU.add))
                    link.then(nc.vector.tensor_reduce(stat[:, 0, :], z[:, :, :], AX.X, ALU.add))
                    link.then(nc.vector.tensor_scalar(stat[:, 0, :], stat[:, 0, :], 1.0 / D, None, ALU.mult))
                    nc.vector.tensor_tensor(z[:, :, :], z[:, :, :], wide_of(stat[:, 0, :]), ALU.subtract).then_inc(centred, 1)

                def variance(i):
                    dve.wait_ge(sq_ready, i + 1)
                    nc.vector.tensor_reduce(stat[:, 1, :], sq[:, :, :], AX.X, ALU.add).then_inc(var_ready, 1)

                def normed(i, k, uses):
                    at = bass.ds(i * PB, PB)
                    dve.wait_ge(std_ready, i + 1)
                    link.then(nc.vector.reciprocal(stat[:, 3, :], stat[:, 2, :]))
                    link.then(nc.vector.tensor_tensor(xs[:, at, :], z[:, :, :], wide_of(stat[:, 3, :]), ALU.mult))
                    if later(uses):
                        dve.wait_ge(y_out[k], 16 * uses)
                    nc.vector.tensor_tensor(y[:, k, :, :], xs[:, at, :], wide_of(count_s[:, at]), ALU.mult).then_inc(y_ready, 1)

                def turn(i, k, uses, front, back, last=False):
                    link.at(SETUP if not back else SETUP + FRONT + (FRONT + BACK) * (i - 1) - (not front))
                    if front:
                        maxima(i)
                        neighbours(i)
                    if front and not last:
                        masks(i + 1)
                    if back:
                        residual(i - 1)
                        variance(i - 1)
                        normed(i - 1, k, uses)
                    assert link.n == (FRONT - last) * front + BACK * back, link.n

                masks(0)
                assert link.n == SETUP
                turn(0, 0, 0, True, False)
                turn(1, 0, 0, True, True)
                turn(2, 1, 0, True, True)
                with dve.Fori(1, pairs // 2 - 1) as h:
                    turn(2 * h + 1, 0, h, True, True)
                    turn(2 * h + 2, 1, h, True, True)
                turn(pairs - 2, 0, pairs // 2 - 1, True, True)
                turn(pairs - 1, 1, pairs // 2 - 1, True, True, last=True)
                turn(pairs, 0, pairs // 2, False, True)

            @block.scalar
            def _(act):
                for k in range(2):
                    act.wait_ge(w_mm, k + 1)
                    last = nc.scalar.copy(wT[64 * k:64 * k + D, :], ps_w[64 * k:64 * k + D, :])
                last.then_inc(w_ready, 1)
                act.wait_ge(eps_ready, 1)

                def carries(i):
                    act.wait_ge(carry_mm, i + 1)
                    nc.scalar.copy(by_group(carry[:, :, :]), in_banks(ps_c, RW)).then_inc(carry_ready, 1)

                def take_rows(g, s, i, last):
                    act.wait_ge(rows_in[s], 16 * GB * (i + 1))
                    nc.scalar.copy(rows[:, s * GB:s * GB + GB, :], landed[:, s, :, :]).then_inc(rows_ready, 1)
                    if not last:
                        act.wait_ge(rows_ready, g + 1)
                        nc.scalar.copy(idx[:, s, :], node_end[:, bass.ds((g + 2) * GB, GB)]).then_inc(staged, 1)

                def exps(i):
                    act.wait_ge(ex_arg, i + 1)
                    nc.scalar.activation(ex[:, :, :], ex_in[:, :, :], ACT.Exp).then_inc(ex_done, 1)

                def transposed(g, s):
                    act.wait_ge(both_t, g + 1)
                    nc.scalar.copy(bothT[:, s, 0:4, :], ps_t[0][:, :, :])
                    nc.scalar.copy(bothT[:, s, 4:GB, :], ps_t[1][:, 0:GB - 4, :]).then_inc(bothT_ready, 1)

                def leaky(g, s):
                    act.wait_ge(prod, g + 1)
                    for k in range(2):
                        last = nc.scalar.mul(part[:, k, s * GB:s * GB + GB, :],
                                             ps_o[k][:, s, 0:GB * D].rearrange("p (b d) -> p b d", d=D), SLOPE)
                    last.then_inc(part_ready, 1)

                def squares(i):
                    act.wait_ge(centred, i + 1)
                    nc.scalar.activation(sq[:, :, :], z[:, :, :], ACT.Square).then_inc(sq_ready, 1)

                def deviations(i):
                    act.wait_ge(var_ready, i + 1)
                    nc.scalar.activation(stat[:, 2, :], stat[:, 1, :], ACT.Sqrt, bias=eps[:, 0:1], scale=1.0 / D).then_inc(std_ready, 1)

                def turn(i, front, back, last=False):
                    if front:
                        exps(i)
                    if back:
                        leaky(2 * i - 2, 0)
                        leaky(2 * i - 1, 1)
                    if front:
                        transposed(2 * i, 0)
                        transposed(2 * i + 1, 1)
                    if back:
                        squares(i - 1)
                        deviations(i - 1)
                    if front and not last:
                        carries(i + 1)
                        take_rows(2 * i + 2, 0, i + 1, last_rows(i))
                        take_rows(2 * i + 3, 1, i + 1, last_rows(i))

                def last_rows(i):
                    return isinstance(i, int) and i == pairs - 2

                carries(0)
                take_rows(0, 0, 0, False)
                take_rows(1, 1, 0, False)
                turn(0, True, False)
                with act.Fori(1, pairs - 2) as i:
                    turn(i, True, True)
                turn(pairs - 2, True, True)
                turn(pairs - 1, True, True, last=True)
                turn(pairs, False, True)

            @block.tensor
            def _(pe):
                pe.wait_ge(w_in, 32)
                nc.tensor.transpose(ps_w[0:D, :], w_raw[:, 0, :], ident[0:D, 0:D]).then_inc(w_mm, 1)
                pe.wait_ge(w_mm, 1)
                nc.tensor.matmul(ps_w[64:64 + D, :], w_raw[:, 1, :], ident[0:D, 0:D], start=True, stop=True).then_inc(w_mm, 1)
                pe.wait_ge(w_ready, 1)

                def carries(i):
                    pe.wait_ge(mask_ready, i + 1)
                    for b in range(PB):
                        at = b % GB * RW
                        last = nc.tensor.matmul(ps_c[:, b // GB, at:at + RW], mask[:, b * P:(b + 1) * P], tail[:, :], start=True, stop=True)
                    last.then_inc(carry_mm, 1)

                def transposes(g, s, i):
                    pe.wait_ge(both_ready, i + 1)
                    if later(g):
                        pe.wait_ge(bothT_ready, g)
                    for b in range(GB):
                        last = nc.tensor.transpose(ps_t[b // 4][:, b % 4, :],
                                                   both[:, s * GB + b, :, :].rearrange("p a d -> p (a d)"), ident[:, :])
                    last.then_inc(both_t, 1)

                def products(g, s, i):
                    pe.wait_ge(bothT_ready, g + 1)
                    if later(i):
                        pe.wait_ge(centred, i)
                    for k in range(2):
                        for b in range(GB):
                            last = nc.tensor.matmul(ps_o[k][:, s, b * D:(b + 1) * D], bothT[64 * k:64 * k + D, s, b, :],
                                                    wT[64 * k:64 * k + D, :], start=True, stop=True)
                    last.then_inc(prod, 1)

                def turn(i, last=False):
                    transposes(2 * i, 0, i)
                    transposes(2 * i + 1, 1, i)
                    if not last:
                        carries(i + 1)
                    products(2 * i, 0, i)
                    products(2 * i + 1, 1, i)

                carries(0)
                turn(0)
                with pe.Fori(1, pairs - 1) as i:
                    turn(i)
                turn(pairs - 1, last=True)


def mean_nodes(nc, sb, ps, sem, xs, iota_row, pool_past, node_end, valid, key, tail, count_d, sums1, out):
    with ExitStack() as c:
        idx = sb(c, "idx_m", [P, 2, GB], I32)
        rows = sb(c, "rows_m", [P, 2, GB, D])
        mask = sb(c, "mask_m", [P, 2, GB * P])
        shifted = sb(c, "shifted_m", [P, 1])
        z = sb(c, "z_m", [P, 2, GB, D])
        sq = sb(c, "sq_m", [P, 2, GB, D])
        stat = sb(c, "stat_m", [P, 2, 4, GB])
        y = sb(c, "y_m", [P, 2, GB, D])
        eps = sb(c, "eps_m", [P, 1])
        ps_c = [ps(c, f"ps_cm{s}", [P, GB, D]) for s in range(2)]
        rows_in = [sem(c, f"rows_inm{s}") for s in range(2)]
        y_out = [sem(c, f"y_outm{s}") for s in range(2)]
        staged, vstep, eps_ready = sem(c, "staged_m"), sem(c, "vstep_m"), sem(c, "eps_ready_m")
        mask_ready, carry_mm = sem(c, "mask_ready_m"), sem(c, "carry_mm_m")
        centred, sq_ready = sem(c, "centred_m"), sem(c, "sq_ready_m")
        var_ready, std_ready, y_ready = sem(c, "var_ready_m"), sem(c, "std_ready_m"), sem(c, "y_ready_m")

        with nc.Block() as block:
            @block.sync
            def _(sp):
                def store(g, s):
                    sp.wait_ge(y_ready, g + 1)
                    sp.dma_start(out[bass.ds(g * GB * P, GB * P), :].rearrange("(b j) d -> j b d", j=P),
                                 y[:, s, :, :]).then_inc(y_out[s], 16)

                with sp.Fori(0, GROUPS // 2 - 1) as i:
                    store(2 * i, 0)
                    store(2 * i + 1, 1)
                store(GROUPS - 2, 0)
                sp.wait_ge(y_ready, GROUPS)
                n0 = (GROUPS - 1) * GB * P
                sp.dma_start(out[n0:n0 + (GB - 1) * P, :].rearrange("(b j) d -> j b d", j=P), y[:, 1, 0:GB - 1, :]).then_inc(y_out[1], 16)
                sp.dma_start(out[(NB - 1) * P:N, :], y[0:TAILROWS, 1, GB - 1, :]).then_inc(y_out[1], 16)
                sp.wait_ge(y_out[0], 16 * (GROUPS // 2))
                sp.wait_ge(y_out[1], 16 * (GROUPS // 2 + 1))

            @block.gpsimd
            def _(pool):
                node_gathers(pool, pool_past, staged, idx, rows, rows_in, sums1)

            @block.vector
            def _(dve):
                link = Steps(dve, vstep)
                SETUP, PER_PAIR = 1, 2 * 8

                def stage(g, s):
                    nc.vector.tensor_copy(idx[:, s, :], node_end[:, bass.ds(g * GB, GB)]).then_inc(staged, 1)

                nc.vector.memset(eps[:, :], EPS).then_inc(eps_ready, 1)
                link.then(nc.vector.tensor_copy(shifted[:, :], key[:, :]))
                stage(0, 0)
                stage(1, 1)

                def masks(g, s, i, last):
                    nc.vector.tensor_scalar(mask[:, s, :], iota_row[:, 0:GB * P], shifted[:, 0:1], None, ALU.is_equal).then_inc(mask_ready, 1)
                    dve.wait_ge(mask_ready, g + 1)
                    link.then(nc.vector.tensor_scalar(shifted[:, :], shifted[:, :], float(-GB * P), None, ALU.add))

                def residual(g, s, i, last):
                    at = bass.ds(g * GB, GB)
                    dve.wait_ge(rows_in[s], 16 * GB * (i + 1))
                    link.then(nc.vector.tensor_tensor(z[:, s, :, :], rows[:, s, :, :], wide_of(valid[:, at]), ALU.mult))
                    if not last:
                        stage(g + 2, s)
                    dve.wait_ge(carry_mm, g + 1)
                    link.then(nc.vector.tensor_tensor(z[:, s, :, :], z[:, s, :, :], ps_c[s][:, :, :], ALU.add))
                    link.then(nc.vector.tensor_tensor(z[:, s, :, :], z[:, s, :, :], wide_of(count_d[:, at]), ALU.mult))
                    link.then(nc.vector.tensor_tensor(z[:, s, :, :], z[:, s, :, :], xs[:, at, :], ALU.add))
                    link.then(nc.vector.tensor_reduce(stat[:, s, 0, :], z[:, s, :, :], AX.X, ALU.add))
                    link.then(nc.vector.tensor_scalar(stat[:, s, 0, :], stat[:, s, 0, :], 1.0 / D, None, ALU.mult))
                    nc.vector.tensor_tensor(z[:, s, :, :], z[:, s, :, :], wide_of(stat[:, s, 0, :]), ALU.subtract).then_inc(centred, 1)

                def variance(g, s, i, last):
                    dve.wait_ge(sq_ready, g + 1)
                    nc.vector.tensor_reduce(stat[:, s, 1, :], sq[:, s, :, :], AX.X, ALU.add).then_inc(var_ready, 1)

                def normed(g, s, i, last):
                    dve.wait_ge(std_ready, g + 1)
                    link.then(nc.vector.reciprocal(stat[:, s, 3, :], stat[:, s, 2, :]))
                    if later(i):
                        dve.wait_ge(y_out[s], 16 * i)
                    nc.vector.tensor_tensor(y[:, s, :, :], z[:, s, :, :], wide_of(stat[:, s, 3, :]), ALU.mult).then_inc(y_ready, 1)

                def pair(i, last):
                    link.at(SETUP + PER_PAIR * i)
                    for step in (masks, residual, variance, normed):
                        step(2 * i, 0, i, last)
                        step(2 * i + 1, 1, i, last)
                    assert link.n == PER_PAIR, link.n

                pair(0, False)
                with dve.Fori(1, GROUPS // 2 - 1) as i:
                    pair(i, False)
                pair(GROUPS // 2 - 1, True)

            @block.scalar
            def _(act):
                act.wait_ge(eps_ready, 1)

                def squares(g, s):
                    act.wait_ge(centred, g + 1)
                    nc.scalar.activation(sq[:, s, :, :], z[:, s, :, :], ACT.Square).then_inc(sq_ready, 1)

                def deviations(g, s):
                    act.wait_ge(var_ready, g + 1)
                    nc.scalar.activation(stat[:, s, 2, :], stat[:, s, 1, :], ACT.Sqrt, bias=eps[:, 0:1], scale=1.0 / D).then_inc(std_ready, 1)

                with act.Fori(0, GROUPS // 2) as i:
                    for step in (squares, deviations):
                        step(2 * i, 0)
                        step(2 * i + 1, 1)

            @block.tensor
            def _(pe):
                def carries(g, s):
                    pe.wait_ge(mask_ready, g + 1)
                    for b in range(GB):
                        last = nc.tensor.matmul(ps_c[s][:, b, :], mask[:, s, b * P:(b + 1) * P], tail[:, 0:D], start=True, stop=True)
                    last.then_inc(carry_mm, 1)

                with pe.Fori(0, GROUPS // 2) as i:
                    carries(2 * i, 0)
                    carries(2 * i + 1, 1)


def gnn_program(nc, x, src, dst, edge_attr, etype, rel_w, res_w1, res_w2, out):
    ctx = ExitStack()
    with ctx:
        def sb(c, name, shape, dt=F32):
            return c.enter_context(nc.sbuf_tensor(name, shape, dt))

        def ps(c, name, shape):
            return c.enter_context(nc.psum_tensor(name, shape, F32))

        def sem(c, name):
            return c.enter_context(nc.semaphore(name))

        table = nc.dram_tensor("table", (NPAD * R, 2 * D), F32).ap()
        sums0 = nc.dram_tensor("sums0", (E, RW), F32).ap()
        sums1 = nc.dram_tensor("sums1", (E, D), F32).ap()
        ytab = nc.dram_tensor("ytab", (NPAD, D), F32).ap()
        table_half = table.rearrange("a (b d) -> (a b) d", b=2)

        xs = sb(ctx, "xs", [P, NB, D])
        src_sb = sb(ctx, "src_sb", [P, T + 2 * G], I32)
        dst_sb = sb(ctx, "dst_sb", [P, 1 + T + 2 * G], I32)
        head_next = sb(ctx, "head_next", [P, 1], I32)
        iota_row = sb(ctx, "iota_row", [P, PB * P])
        iota_col = sb(ctx, "iota_col", [P, 1])
        ident = sb(ctx, "ident", [P, P])
        count_d = sb(ctx, "count_d", [P, NB])
        count_s = sb(ctx, "count_s", [P, NB])
        node_end = sb(ctx, "node_end", [P, NB], I32)
        valid = sb(ctx, "valid", [P, NB])
        key = sb(ctx, "key", [P, 1])
        tail = sb(ctx, "tail", [P, RW])

        with ExitStack() as c1:
            SLOTS = 4
            POOL_DUP, ACT_DUP = 8, 8
            w_all = sb(c1, "w_all", [P, R, D])
            rows = sb(c1, "rows", [P, SLOTS, R, 2 * D])
            xb = sb(c1, "xb", [P, 2, D])
            xbT = sb(c1, "xbT", [P, SLOTS, P])
            ps_x = [ps(c1, f"ps_x{k}", [P, P]) for k in range(2)]
            QUART = R * D // 4
            ps_p = [ps(c1, f"ps_p{k}", [P, QUART]) for k in range(4)]
            x_in, x_zero, w_zero = sem(c1, "x_in"), sem(c1, "x_zero"), sem(c1, "w_zero")
            w_in, idx_in, idx_pad = sem(c1, "w_in"), sem(c1, "idx_in"), sem(c1, "idx_pad")
            iota_done, const_done = sem(c1, "iota_done"), sem(c1, "const_done")
            xb_ready, xT_ready, xbT_ready = sem(c1, "xb_ready"), sem(c1, "xT_ready"), sem(c1, "xbT_ready")
            proj_ready = [sem(c1, f"proj_ready{k}") for k in range(4)]
            taken = [sem(c1, f"taken{k}") for k in range(4)]
            dup_ready = sem(c1, "dup_ready")
            stored = [sem(c1, f"stored{s}") for s in range(SLOTS)]
            pool_past, pe_past = sem(ctx, "pool_past"), sem(c1, "pe_past")

            def each_block(engine, step):
                for b in range(SLOTS):
                    step(b, b, 0)
                with engine.Fori(1, NB // SLOTS) as i:
                    for s in range(SLOTS):
                        step(SLOTS * i + s, s, i)
                for b in range(NB // SLOTS * SLOTS, NB):
                    step(b, b % SLOTS, b // SLOTS)

            with nc.Block() as block:
                @block.sync
                def _(sp):
                    sp.wait_ge(x_zero, 1)
                    sp.dma_start(xs[:, 0:NB - 1, :], x[0:(NB - 1) * P, :].rearrange("(b j) d -> j b d", j=P)).then_inc(x_in, 16)
                    sp.dma_start(xs[0:TAILROWS, NB - 1, :], x[(NB - 1) * P:N, :]).then_inc(x_in, 16)
                    sp.dma_start(w_all[0:D, :, :], rel_w.rearrange("r d e -> d r e")).then_inc(w_in, 16)
                    sp.wait_ge(idx_pad, 4)
                    sp.dma_start(src_sb[:, 0:T], src.rearrange("(p t) -> p t", p=P)).then_inc(idx_in, 16)
                    sp.dma_start(dst_sb[:, 1:1 + T], dst.rearrange("(p t) -> p t", p=P)).then_inc(idx_in, 16)
                    with nc.allow_non_contiguous_dma(reason="one number of each partition"):
                        sp.dma_start(head_next[0:P - 1, :], dst[T:E].rearrange("(p t) -> p t", p=P - 1)[:, 0:1]).then_inc(idx_in, 16)

                    def store(b, s, i):
                        sp.wait_ge(dup_ready, b + 1)
                        for k in range(4):
                            sp.wait_ge(taken[k], b + 1)
                        sp.dma_start(table[bass.ds(b * P * R, P * R), :].rearrange("(j r) c -> j (r c)", r=R),
                                     rows[:, s, :, :].rearrange("p r c -> p (r c)")).then_inc(stored[s], 16)

                    each_block(sp, store)
                    for s in range(SLOTS):
                        sp.wait_ge(stored[s], 16 * len(range(s, NB, SLOTS)))
                    sp.wait_ge(idx_in, 48)

                @block.gpsimd
                def _(pool):
                    pool.iota(iota_row[:, :], [[1, PB * P]], base=0, channel_multiplier=0,
                              allow_small_or_imprecise_dtypes=True).then_inc(iota_done, 1)
                    pool.iota(iota_col[:, :], [[0, 1]], base=0, channel_multiplier=1,
                              allow_small_or_imprecise_dtypes=True).then_inc(iota_done, 1)
                    pool.wait_ge(x_in, 32)

                    def duplicate(b, s, i):
                        if later(b):
                            pool.wait_ge(xbT_ready, b)
                        pool.sem_inc(pool_past, 1)
                        pool.tensor_copy(xb[:, :, :], xs[:, bass.ds(b, 1), :].to_broadcast([P, 2, D])).then_inc(xb_ready, 1)
                        if later(i):
                            pool.wait_ge(stored[s], 16 * i)
                        pool.sem_inc(pool_past, 1)
                        pool.tensor_copy(rows[:, s, R - POOL_DUP:R, D:2 * D],
                                         xs[:, bass.ds(b, 1), :].to_broadcast([P, POOL_DUP, D])).then_inc(dup_ready, 1)

                    each_block(pool, duplicate)

                @block.tensor
                def _(pe):
                    pe.wait_ge(const_done, 1)
                    pe.wait_ge(w_zero, 1)
                    pe.wait_ge(w_in, 16)

                    def transpose_x(b, k):
                        pe.wait_ge(xb_ready, b + 1)
                        pe.sem_inc(pe_past, 1)
                        nc.tensor.transpose(ps_x[k][:, :], xb[:, :, :].rearrange("p a d -> p (a d)"), ident[:, :]).then_inc(xT_ready, 1)

                    def project(b, s, i):
                        if not (isinstance(b, int) and b == NB - 1):
                            transpose_x(b + 1, (s + 1) % 2)
                        pe.wait_ge(xbT_ready, b + 1)
                        for k in range(4):
                            if later(b):
                                pe.wait_ge(taken[k], b)
                            nc.tensor.matmul(ps_p[k][:, :], xbT[:, s, :],
                                             w_all[:, k * R // 4:(k + 1) * R // 4, :].rearrange("d r e -> d (r e)"),
                                             start=True, stop=True).then_inc(proj_ready[k], 1)

                    transpose_x(0, 0)
                    each_block(pe, project)

                def take_out(engine, copy, k, b, s, i):
                    engine.wait_ge(proj_ready[k], b + 1)
                    if later(i):
                        engine.wait_ge(stored[s], 16 * i)
                    copy(rows[:, s, k * R // 4:(k + 1) * R // 4, 0:D],
                         ps_p[k][:, :].rearrange("p (r e) -> p r e", e=D)).then_inc(taken[k], 1)

                @block.vector
                def _(dve):
                    nc.vector.memset(xs[:, NB - 1, :], 0.0).then_inc(x_zero, 1)
                    nc.vector.memset(w_all[D:P, :, :], 0.0).then_inc(w_zero, 1)
                    nc.vector.memset(src_sb[:, T:], 0).then_inc(idx_pad, 1)
                    nc.vector.memset(dst_sb[:, 0:1], -1).then_inc(idx_pad, 1)
                    nc.vector.memset(dst_sb[:, 1 + T:], 0).then_inc(idx_pad, 1)
                    nc.vector.memset(head_next[:, :], -1).then_inc(idx_pad, 1)
                    dve.wait_ge(x_in, 32)
                    dve.wait_ge(iota_done, 2)
                    nc.vector.tensor_scalar(ident[:, :], iota_row[:, 0:P], iota_col[:, 0:1], None, ALU.is_equal).then_inc(const_done, 1)

                    def quarters(b, s, i):
                        take_out(dve, nc.vector.tensor_copy, 0, b, s, i)
                        nc.vector.tensor_copy(rows[:, s, 0:R - POOL_DUP - ACT_DUP, D:2 * D],
                                              xs[:, bass.ds(b, 1), :].to_broadcast([P, R - POOL_DUP - ACT_DUP, D]))
                        take_out(dve, nc.vector.tensor_copy, 2, b, s, i)

                    each_block(dve, quarters)

                @block.scalar
                def _(act):
                    act.wait_ge(x_in, 32)

                    def take_x(b, k, s):
                        act.wait_ge(xT_ready, b + 1)
                        nc.scalar.copy(xbT[:, s, :], ps_x[k][:, :]).then_inc(xbT_ready, 1)

                    def quarters(b, s, i):
                        if not (isinstance(b, int) and b == NB - 1):
                            take_x(b + 1, (s + 1) % 2, (s + 1) % SLOTS)
                        take_out(act, nc.scalar.copy, 1, b, s, i)
                        nc.scalar.copy(rows[:, s, R - POOL_DUP - ACT_DUP:R - POOL_DUP, D:2 * D],
                                       xs[:, bass.ds(b, 1), :].to_broadcast([P, ACT_DUP, D]))
                        take_out(act, nc.scalar.copy, 3, b, s, i)

                    take_x(0, 0, 0)
                    each_block(act, quarters)

        with ExitStack() as c2:
            type_sb = sb(c2, "type_sb", [P, T + 2 * G], I32)
            idx_s = sb(c2, "idx_s", [P, 2, G], I32)
            idx_d = sb(c2, "idx_d", [P, 2, G], I32)
            gs = sb(c2, "gs", [P, 2, G, 2 * D])
            gd = sb(c2, "gd", [P, 2, G, D])
            ef = sb(c2, "ef", [P, 2, G, D])
            att = sb(c2, "att", [P, G])
            same = sb(c2, "same", [P, G])
            gap = sb(c2, "gap", [P, G])
            mx = sb(c2, "mx", [P, 1 + G])
            ex_in = sb(c2, "ex_in", [P, 2, G])
            ex = sb(c2, "ex", [P, 2, G])
            keep = sb(c2, "keep", [P, W, 1 + G])
            add = sb(c2, "add", [P, W, 1 + G])
            run = sb(c2, "run", [P, W, 1 + G])
            rowbuf = sb(c2, "rowbuf", [P, 2, G, RW])
            digit = sb(c2, "digit", [P, 4, G], I32)
            lo_s = sb(c2, "lo_s", [P, G, P], BF16)
            lo_d = sb(c2, "lo_d", [P, G, P], BF16)
            hi_s = sb(c2, "hi_s", [P, G, NB], BF16)
            hi_d = sb(c2, "hi_d", [P, G, NB], BF16)
            zero = sb(c2, "zero", [P, P], BF16)
            hist_s, hist_d = ps(c2, "hist_s", [P, NB]), ps(c2, "hist_d", [P, NB])
            type_in, type_pad = sem(c2, "type_in"), sem(c2, "type_pad")
            ef_in = [sem(c2, f"ef_in{s}") for s in range(2)]
            gs_in = [sem(c2, f"gs_in{s}") for s in range(2)]
            gd_in = [sem(c2, f"gd_in{s}") for s in range(2)]
            stored = [sem(c2, f"rows_stored{s}") for s in range(2)]
            vstep = sem(c2, "vstep")
            slot_ready = sem(c2, "slot_ready")
            tanh_arg, tanh_done = sem(c2, "tanh_arg"), sem(c2, "tanh_done")
            exp_arg, exp_done = sem(c2, "exp_arg"), sem(c2, "exp_done")
            keep_ready, run_ready, rows_ready = sem(c2, "keep_ready"), sem(c2, "run_ready"), sem(c2, "rows_ready")
            onehot_ready, onehot_used = sem(c2, "onehot_ready"), sem(c2, "onehot_used")
            hist_begun, hist_done, init_done = sem(c2, "hist_begun"), sem(c2, "hist_done"), sem(c2, "init_done")
            edges = edge_attr.rearrange("(p t) d -> p t d", p=P)
            sums0_v = sums0.rearrange("(p t) w -> p t w", p=P)

            with nc.Block() as block:
                @block.sync
                def _(sp):
                    sp.wait_ge(type_pad, 1)
                    sp.dma_start(type_sb[:, 0:T], etype.rearrange("(p t) -> p t", p=P)).then_inc(type_in, 16)

                    def load(c, s):
                        sp.dma_start(ef[:, s, :, :], edges[:, bass.ds(c * G, G), :]).then_inc(ef_in[s], 16)

                    load(0, 0)
                    load(1, 1)
                    with sp.Fori(0, PAIRS - 1) as i:
                        sp.wait_ge(tanh_arg, 2 * i + 1)
                        load(2 * i + 2, 0)
                        sp.wait_ge(tanh_arg, 2 * i + 2)
                        load(2 * i + 3, 1)
                    sp.wait_ge(tanh_arg, CHUNKS - 2)
                    load(CHUNKS - 1, 0)

                @block.gpsimd
                def _(pool):
                    def gather(c, s):
                        pool.wait_ge(slot_ready, c + 1)
                        pool.sem_inc(pool_past, 1)
                        for g in range(G):
                            pool.indirect_dma_start(
                                out=gs[:, s, g, :], out_offset=None, in_=table,
                                in_offset=bass.IndirectOffsetOnAxis(ap=idx_s[:, s, g:g + 1], axis=0)).then_inc(gs_in[s], 16)
                            pool.indirect_dma_start(
                                out=gd[:, s, g, :], out_offset=None, in_=table_half,
                                in_offset=bass.IndirectOffsetOnAxis(ap=idx_d[:, s, g:g + 1], axis=0)).then_inc(gd_in[s], 16)

                    with pool.Fori(0, PAIRS) as i:
                        gather(2 * i, 0)
                        gather(2 * i + 1, 1)
                    gather(CHUNKS - 1, 0)

                @block.vector
                def _(dve):
                    link = Steps(dve, vstep)
                    SETUP, PER_CHUNK = 6, 13

                    def stage(c, s):
                        at = bass.ds(c * G, G)
                        at_d = bass.ds(c * G + 1, G)
                        nc.vector.scalar_tensor_tensor(out=idx_s[:, s, :], in0=src_sb[:, at], scalar=float(R),
                                                       in1=type_sb[:, at], op0=ALU.mult, op1=ALU.add)
                        link.then(nc.vector.scalar_tensor_tensor(out=idx_d[:, s, :], in0=dst_sb[:, at_d], scalar=float(R),
                                                                 in1=type_sb[:, at], op0=ALU.mult, op1=ALU.add))
                        nc.vector.tensor_scalar(idx_d[:, s, :], idx_d[:, s, :], 2.0, None, ALU.mult).then_inc(slot_ready, 1)

                    nc.vector.memset(type_sb[:, T:], 0).then_inc(type_pad, 1)
                    nc.vector.memset(zero[:, :], 0.0).then_inc(init_done, 1)
                    link.then(nc.vector.memset(digit[:, :, :], 0))
                    link.then(nc.vector.memset(mx[:, :], -BIG))
                    link.then(nc.vector.memset(keep[:, :, :], 0.0))
                    link.then(nc.vector.memset(run[:, :, :], 0.0))
                    nc.vector.memset(add[:, :, :], 0.0).then_inc(init_done, 1)
                    dve.wait_ge(type_in, 16)
                    stage(0, 0)
                    stage(1, 1)
                    assert link.n == SETUP

                    def chunk(c, s, i):
                        link.at(SETUP + c * PER_CHUNK)
                        at = bass.ds(c * G, G)
                        at_d = bass.ds(c * G + 1, G)
                        nc.vector.tensor_scalar(digit[:, 0, :], src_sb[:, at], 127, None, ALU.bitwise_and)
                        nc.vector.tensor_scalar(digit[:, 1, :], src_sb[:, at], 7, None, ALU.logical_shift_right)
                        nc.vector.tensor_scalar(digit[:, 2, :], dst_sb[:, at_d], 127, None, ALU.bitwise_and)
                        link.then(nc.vector.tensor_scalar(digit[:, 3, :], dst_sb[:, at_d], 7, None, ALU.logical_shift_right))
                        if later(c):
                            dve.wait_ge(onehot_used, c)
                        for k, (hot, width) in enumerate(((lo_s, P), (hi_s, NB), (lo_d, P), (hi_d, NB))):
                            last = nc.vector.tensor_tensor(
                                hot[:, :, :], iota_row[:, 0:width].unsqueeze(1).to_broadcast([P, G, width]),
                                digit[:, k, :].unsqueeze(2).to_broadcast([P, G, width]), ALU.is_equal)
                        last.then_inc(onehot_ready, 1)
                        link.then(nc.vector.tensor_tensor(same[:, :], dst_sb[:, at_d], dst_sb[:, at], ALU.is_equal))
                        link.then(nc.vector.tensor_scalar(gap[:, :], same[:, :], -1.0, BIG, ALU.add, ALU.mult))
                        dve.wait_ge(ef_in[s], 16 * (i + 1))
                        dve.wait_ge(gd_in[s], 16 * G * (i + 1))
                        nc.vector.tensor_tensor(gd[:, s, :, :], gd[:, s, :, :], ef[:, s, :, :], ALU.add).then_inc(tanh_arg, 1)
                        dve.wait_ge(gs_in[s], 16 * G * (i + 1))
                        dve.wait_ge(tanh_done, c + 1)
                        link.then(nc.vector.tensor_tensor(gd[:, s, :, :], gd[:, s, :, :], gs[:, s, :, 0:D], ALU.mult))
                        link.then(nc.vector.tensor_reduce(att[:, :], gd[:, s, :, :], AX.X, ALU.add))
                        if later(c):
                            dve.wait_ge(rows_ready, c)
                        link.then(nc.vector.tensor_copy(mx[:, 0:1], mx[:, G:G + 1]))
                        link.then(nc.vector.tensor_tensor_scan(mx[:, 1:], gap[:, :], att[:, :], mx[:, 0:1], ALU.add, ALU.max))
                        link.then(nc.vector.tensor_tensor(ex_in[:, 0, :], att[:, :], mx[:, 1:], ALU.subtract))
                        link.then(nc.vector.tensor_tensor(ex_in[:, 1, :], mx[:, 0:G], gap[:, :], ALU.add))
                        nc.vector.tensor_tensor(ex_in[:, 1, :], ex_in[:, 1, :], mx[:, 1:], ALU.subtract).then_inc(exp_arg, 1)
                        link.then(nc.vector.tensor_copy(add[:, :, 0], run[:, :, G]))
                        dve.wait_ge(exp_done, c + 1)
                        link.then(nc.vector.tensor_copy(add[:, D, 1:], ex[:, 0, :]))
                        link.then(nc.vector.tensor_tensor(
                            add[:, 0:D, 1:].rearrange("p d t -> p t d"), gs[:, s, :, D:2 * D],
                            ex[:, 0, :].unsqueeze(2).to_broadcast([P, G, D]), ALU.mult))
                        dve.wait_ge(keep_ready, c + 1)
                        nc.vector.tensor_tensor_scan(run[:, :, :].rearrange("p w t -> p (w t)"),
                                                     keep[:, :, :].rearrange("p w t -> p (w t)"),
                                                     add[:, :, :].rearrange("p w t -> p (w t)"),
                                                     0.0, ALU.mult, ALU.add).then_inc(run_ready, 1)
                        stage(c + 2, s)
                        assert link.n == PER_CHUNK, link.n

                    chunk(0, 0, 0)
                    chunk(1, 1, 0)
                    with dve.Fori(1, PAIRS) as i:
                        chunk(2 * i, 0, i)
                        chunk(2 * i + 1, 1, i)
                    chunk(CHUNKS - 1, 0, PAIRS)
                    dve.wait_ge(hist_done, 1)
                    nc.vector.tensor_copy(count_s[:, :], hist_s[:, :])
                    nc.vector.tensor_copy(count_d[:, :], hist_d[:, :])
                    nc.vector.tensor_copy(tail[:, 0:W], run[:, :, G])
                    nc.vector.tensor_copy(tail[:, W:RW], mx[:, G:G + 1])

                @block.scalar
                def _(act):
                    act.wait_ge(init_done, 2)

                    def chunk(c, s, i):
                        act.wait_ge(tanh_arg, c + 1)
                        nc.scalar.activation(gd[:, s, :, :], gd[:, s, :, :], ACT.Tanh).then_inc(tanh_done, 1)
                        act.wait_ge(exp_arg, c + 1)
                        nc.scalar.activation(ex[:, :, :], ex_in[:, :, :], ACT.Exp).then_inc(exp_done, 1)
                        act.wait_ge(exp_done, c + 1)
                        nc.scalar.copy(keep[:, :, 1:], ex[:, 1, :].unsqueeze(1).to_broadcast([P, W, G])).then_inc(keep_ready, 1)
                        act.wait_ge(run_ready, c + 1)
                        if later(i):
                            act.wait_ge(stored[s], 16 * i)
                        nc.scalar.copy(rowbuf[:, s, :, 0:W], run[:, :, 1:].rearrange("p w t -> p t w"))
                        nc.scalar.copy(rowbuf[:, s, :, W], mx[:, 1:]).then_inc(rows_ready, 1)
                        act.wait_ge(rows_ready, c + 1)
                        act.dma_start(sums0_v[:, bass.ds(c * G, G), :], rowbuf[:, s, :, :]).then_inc(stored[s], 16)

                    chunk(0, 0, 0)
                    chunk(1, 1, 0)
                    with act.Fori(1, PAIRS) as i:
                        chunk(2 * i, 0, i)
                        chunk(2 * i + 1, 1, i)
                    chunk(CHUNKS - 1, 0, PAIRS)
                    act.wait_ge(stored[0], 16 * (PAIRS + 1))
                    act.wait_ge(stored[1], 16 * PAIRS)

                @block.tensor
                def _(pe):
                    pe.wait_ge(init_done, 1)
                    nc.tensor.matmul(hist_s[:, :], zero[:, :], zero[:, 0:NB], start=True, stop=False)
                    nc.tensor.matmul(hist_d[:, :], zero[:, :], zero[:, 0:NB], start=True, stop=False)
                    with pe.Fori(0, CHUNKS) as c:
                        pe.wait_ge(onehot_ready, c + 1)
                        for g in range(G):
                            nc.tensor.matmul(hist_s[:, :], lo_s[:, g, :], hi_s[:, g, :], start=False, stop=False)
                            last = nc.tensor.matmul(hist_d[:, :], lo_d[:, g, :], hi_d[:, g, :], start=False, stop=False)
                        last.then_inc(onehot_used, 1)
                    nc.tensor.matmul(hist_s[:, :], zero[:, :], zero[:, 0:NB], start=False, stop=True)
                    nc.tensor.matmul(hist_d[:, :], zero[:, :], zero[:, 0:NB], start=False, stop=True).then_inc(hist_done, 1)

        tail_stage(nc, sb, ps, sem, dst_sb, head_next, iota_row, iota_col, ident, count_d, count_s,
                   node_end, valid, key, tail)
        attention_nodes(nc, sb, ps, sem, res_w1, res_w2, xs, ident, iota_row, pool_past, node_end, valid, key, tail,
                        count_s, sums0, ytab)

        with ExitStack() as c4:
            idx = sb(c4, "idx", [P, 2, G], I32)
            gy = sb(c4, "gy", [P, 2, G, D])
            same = sb(c4, "same1", [P, G])
            keep = sb(c4, "keep1", [P, D, 1 + G])
            add = sb(c4, "add1", [P, D, 1 + G])
            run = sb(c4, "run1", [P, D, 1 + G])
            rowbuf = sb(c4, "rowbuf1", [P, 2, G, D])
            gy_in = [sem(c4, f"gy_in{s}") for s in range(2)]
            stored = [sem(c4, f"rows1_stored{s}") for s in range(2)]
            slot_ready, same_ready = sem(c4, "slot1_ready"), sem(c4, "same_ready")
            keep_ready, run_ready = sem(c4, "keep1_ready"), sem(c4, "run1_ready")
            rows_ready, init_done, vstep = sem(c4, "rows1_ready"), sem(c4, "init1_done"), sem(c4, "vstep1")
            sums1_v = sums1.rearrange("(p t) w -> p t w", p=P)

            with nc.Block() as block:
                @block.gpsimd
                def _(pool):
                    def gather(c, s):
                        pool.wait_ge(slot_ready, c + 1)
                        pool.sem_inc(pool_past, 1)
                        for g in range(G):
                            pool.indirect_dma_start(
                                out=gy[:, s, g, :], out_offset=None, in_=ytab,
                                in_offset=bass.IndirectOffsetOnAxis(ap=idx[:, s, g:g + 1], axis=0)).then_inc(gy_in[s], 16)

                    with pool.Fori(0, PAIRS) as i:
                        gather(2 * i, 0)
                        gather(2 * i + 1, 1)
                    gather(CHUNKS - 1, 0)

                @block.vector
                def _(dve):
                    link = Steps(dve, vstep)

                    def stage(c, s):
                        nc.vector.tensor_copy(idx[:, s, :], src_sb[:, bass.ds(c * G, G)]).then_inc(slot_ready, 1)

                    nc.vector.memset(keep[:, :, :], 0.0).then_inc(init_done, 1)
                    nc.vector.memset(add[:, :, :], 0.0).then_inc(init_done, 1)
                    link.then(nc.vector.memset(run[:, :, :], 0.0))
                    stage(0, 0)
                    stage(1, 1)

                    def chunk(c, s, i):
                        link.at(1 + c)
                        if later(c):
                            dve.wait_ge(keep_ready, c)
                        nc.vector.tensor_tensor(same[:, :], dst_sb[:, bass.ds(c * G + 1, G)], dst_sb[:, bass.ds(c * G, G)],
                                                ALU.is_equal).then_inc(same_ready, 1)
                        if later(c):
                            dve.wait_ge(rows_ready, c)
                        link.then(nc.vector.tensor_copy(add[:, :, 0], run[:, :, G]))
                        dve.wait_ge(gy_in[s], 16 * G * (i + 1))
                        dve.wait_ge(keep_ready, c + 1)
                        nc.vector.tensor_tensor_scan(run[:, :, :].rearrange("p w t -> p (w t)"),
                                                     keep[:, :, :].rearrange("p w t -> p (w t)"),
                                                     add[:, :, :].rearrange("p w t -> p (w t)"),
                                                     0.0, ALU.mult, ALU.add).then_inc(run_ready, 1)
                        stage(c + 2, s)

                    chunk(0, 0, 0)
                    chunk(1, 1, 0)
                    with dve.Fori(1, PAIRS) as i:
                        chunk(2 * i, 0, i)
                        chunk(2 * i + 1, 1, i)
                    chunk(CHUNKS - 1, 0, PAIRS)
                    dve.wait_ge(run_ready, CHUNKS)
                    nc.vector.tensor_copy(tail[:, 0:D], run[:, :, G])

                @block.scalar
                def _(act):
                    act.wait_ge(init_done, 2)

                    def chunk(c, s, i):
                        act.wait_ge(gy_in[s], 16 * G * (i + 1))
                        nc.scalar.copy(add[:, :, 1:].rearrange("p d t -> p t d"), gy[:, s, :, :])
                        act.wait_ge(same_ready, c + 1)
                        nc.scalar.copy(keep[:, :, 1:], same[:, :].unsqueeze(1).to_broadcast([P, D, G])).then_inc(keep_ready, 1)
                        act.wait_ge(run_ready, c + 1)
                        if later(i):
                            act.wait_ge(stored[s], 16 * i)
                        nc.scalar.copy(rowbuf[:, s, :, :], run[:, :, 1:].rearrange("p w t -> p t w")).then_inc(rows_ready, 1)
                        act.wait_ge(rows_ready, c + 1)
                        act.dma_start(sums1_v[:, bass.ds(c * G, G), :], rowbuf[:, s, :, :]).then_inc(stored[s], 16)

                    chunk(0, 0, 0)
                    chunk(1, 1, 0)
                    with act.Fori(1, PAIRS) as i:
                        chunk(2 * i, 0, i)
                        chunk(2 * i + 1, 1, i)
                    chunk(CHUNKS - 1, 0, PAIRS)
                    act.wait_ge(stored[0], 16 * (PAIRS + 1))
                    act.wait_ge(stored[1], 16 * PAIRS)

        mean_nodes(nc, sb, ps, sem, xs, iota_row, pool_past, node_end, valid, key, tail, count_d, sums1, out)


_INS = ['x', 'src', 'dst', 'edge_attr_64', 'edge_type_32', 'L0_gnn_relation_weight', 'L0_gnn_res_w1', 'L0_gnn_res_w2']
_OUTS = [((N, D), 'float32')]


def kernel(**inputs):
    import numpy as _np
    import concourse.bacc as _bacc
    from concourse import mybir as _mybir
    from concourse.bass_utils import run_bass_kernel_spmd as _run

    nc = _bacc.Bacc("TRN2", target_bir_lowering=False, num_devices=1)
    arrays, args = {}, []
    for name in _INS:
        a = _np.ascontiguousarray(inputs[name])
        arrays[f"in_{name}_dram"] = a
        args.append(nc.dram_tensor(f"in_{name}_dram", a.shape, _mybir.dt.from_np(a.dtype), kind="ExternalInput").ap())
    for i, (shape, dtype) in enumerate(_OUTS):
        dt = _mybir.dt.from_np(_np.dtype(dtype))
        args.append(nc.dram_tensor(f"out_{i}_dram", shape, dt, kind="ExternalOutput").ap())
    gnn_program(nc, *args)
    r = _run(nc, [arrays], core_ids=[0])
    return r.results[0]["out_0_dram"]
```
